# Optimizing a Trainium2 kernel written in Bass

```python
import numpy as np
import jax
import jax.numpy as jnp

def _softmax(x, axis=-1):
    return jax.nn.softmax(x, axis=axis)

def _gelu(x):
    return jax.nn.gelu(x, approximate=True)

def _silu(x):
    return jax.nn.silu(x)

def _sigmoid(x):
    return jax.nn.sigmoid(x)

def _layernorm(x, axis=-1, eps=1e-05):
    m = jnp.mean(x, axis=axis, keepdims=True)
    v = jnp.var(x, axis=axis, keepdims=True)
    return (x - m) / jnp.sqrt(v + eps)

def _scatter_add(tgt, idx, src, axis=0):
    return tgt.at[idx].add(src)

def _segment_sum(src, seg, n):
    return jax.ops.segment_sum(src, seg, n)
kernel_name = 'mk_xattn_seq_d2_seqx_r4_41390c'

def setup_inputs(seed: int=0):
    np.random.seed(seed)
    _w = jnp.asarray

    def _rec_inputs():
        import jax
        import jax.numpy as jnp
        _rk = jax.random.key(seed)
        x = -0.000125 + 0.9999 * jax.random.normal(jax.random.fold_in(_rk, 1), (32, 128, 1024), jnp.float32)
        _lenS = 128 - jax.random.randint(jax.random.fold_in(_rk, 7), (32,), 0, max(1, 128 // 4) + 1, jnp.int32)
        _lenS2 = 128 - jax.random.randint(jax.random.fold_in(_rk, 8), (32,), 0, max(1, 128 // 4) + 1, jnp.int32)
        _ctx_4096P = jax.random.normal(jax.random.fold_in(_rk, 11), (32, 16, 1024), jnp.float32)
        _ctx_4096c = jax.random.dirichlet(jax.random.fold_in(_rk, 511), 0.3 * jnp.ones((16,), jnp.float32), (32, 128))
        _ctx_4096t = jnp.einsum('bsk,bkd->bsd', _ctx_4096c, _ctx_4096P)
        _ctx_4096t = _ctx_4096t * jax.lax.rsqrt(jnp.mean(jnp.square(_ctx_4096t)) + 1e-12) * 0.953939
        ctx_4096 = -1.52775e-05 + 0.999936 * (_ctx_4096t + 0.3 * jax.random.normal(jax.random.fold_in(_rk, 611), (32, 128, 1024), jnp.float32))
        return (x, ctx_4096)
    x, ctx_4096 = _rec_inputs()

    def _L0_xattn_setup():
        import jax, jax.numpy as jnp
        import numpy as np
        NUM_HEADS = 8
        EPS = 1e-05

        def _conv1x1(W, b, t):
            return jnp.einsum('oc,bcl->bol', W, t) + b[None, :, None]
        key = jax.random.key(seed)
        ks = jax.random.split(key, 12)
        B, C, E, L = (16, 128, 128, 1024)
        s = lambda k, shape, sc=1.0: jax.random.normal(k, shape, dtype=jnp.float32) * sc
        return {'x': s(ks[0], (B, E, L)), 'y': s(ks[1], (B, C, L)), 'Wq': s(ks[2], (E, C), 0.02), 'bq': jnp.zeros((E,), jnp.float32), 'Wk': s(ks[3], (E, C), 0.02), 'bk': jnp.zeros((E,), jnp.float32), 'Wv': s(ks[4], (E, E), 0.02), 'bv': jnp.zeros((E,), jnp.float32), 'Wo': s(ks[5], (E, E), 0.02), 'bo': jnp.zeros((E,), jnp.float32), 'gn_w': jnp.ones((E,), jnp.float32), 'gn_b': jnp.zeros((E,), jnp.float32)}
    _L0_xattn_all = _L0_xattn_setup()
    _L0_xattn_in = {k: v for k, v in _L0_xattn_all.items() if k in ('Wq', 'bq', 'Wk', 'bk', 'Wv', 'bv', 'Wo', 'bo', 'gn_w', 'gn_b')}
    del _L0_xattn_all

    def _L1_xattn_setup():
        import jax, jax.numpy as jnp
        import numpy as np
        H = 1024
        NH = 32
        NKV = 8
        HD = H // NH
        R = 16
        SCALING = 32.0 / 16.0

        def _lora_linear(x, W, A, B):
            return x @ W + SCALING * (x @ A @ B)
        key = jax.random.key(seed)
        ks = jax.random.split(key, 16)
        d = {'hidden_states': jax.random.normal(ks[0], (4, 256, H), jnp.float32), 'traces': jax.random.normal(ks[1], (4, 256, H), jnp.float32), 'Wq': jax.random.normal(ks[2], (H, H), jnp.float32) * 0.02, 'Aq': jax.random.normal(ks[3], (H, R), jnp.float32) * 0.02, 'Bq': jax.random.normal(ks[4], (R, H), jnp.float32) * 0.02, 'Wk': jax.random.normal(ks[5], (H, NKV * HD), jnp.float32) * 0.02, 'Ak': jax.random.normal(ks[6], (H, R), jnp.float32) * 0.02, 'Bk': jax.random.normal(ks[7], (R, NKV * HD), jnp.float32) * 0.02, 'Wv': jax.random.normal(ks[8], (H, NKV * HD), jnp.float32) * 0.02, 'Av': jax.random.normal(ks[9], (H, R), jnp.float32) * 0.02, 'Bv': jax.random.normal(ks[10], (R, NKV * HD), jnp.float32) * 0.02, 'Wo': jax.random.normal(ks[11], (H, H), jnp.float32) * 0.02, 'Ao': jax.random.normal(ks[12], (H, R), jnp.float32) * 0.02, 'Bo': jax.random.normal(ks[13], (R, H), jnp.float32) * 0.02}
        return d
    _L1_xattn_all = _L1_xattn_setup()
    _L1_xattn_in = {k: v for k, v in _L1_xattn_all.items() if k in ('Wq', 'Aq', 'Bq', 'Wk', 'Ak', 'Bk', 'Wv', 'Av', 'Bv', 'Wo', 'Ao', 'Bo')}
    del _L1_xattn_all
    return {'x': x, 'ctx_4096': ctx_4096, 'L0_xattn_Wq': _L0_xattn_in['Wq'], 'L0_xattn_bq': _L0_xattn_in['bq'], 'L0_xattn_Wk': _L0_xattn_in['Wk'], 'L0_xattn_bk': _L0_xattn_in['bk'], 'L0_xattn_Wv': _L0_xattn_in['Wv'], 'L0_xattn_bv': _L0_xattn_in['bv'], 'L0_xattn_Wo': _L0_xattn_in['Wo'], 'L0_xattn_bo': _L0_xattn_in['bo'], 'L0_xattn_gn_w': _L0_xattn_in['gn_w'], 'L0_xattn_gn_b': _L0_xattn_in['gn_b'], 'L1_xattn_Wq': _L1_xattn_in['Wq'], 'L1_xattn_Aq': _L1_xattn_in['Aq'], 'L1_xattn_Bq': _L1_xattn_in['Bq'], 'L1_xattn_Wk': _L1_xattn_in['Wk'], 'L1_xattn_Ak': _L1_xattn_in['Ak'], 'L1_xattn_Bk': _L1_xattn_in['Bk'], 'L1_xattn_Wv': _L1_xattn_in['Wv'], 'L1_xattn_Av': _L1_xattn_in['Av'], 'L1_xattn_Bv': _L1_xattn_in['Bv'], 'L1_xattn_Wo': _L1_xattn_in['Wo'], 'L1_xattn_Ao': _L1_xattn_in['Ao'], 'L1_xattn_Bo': _L1_xattn_in['Bo']}

def reference(x, ctx_4096, L0_xattn_Wq, L0_xattn_bq, L0_xattn_Wk, L0_xattn_bk, L0_xattn_Wv, L0_xattn_bv, L0_xattn_Wo, L0_xattn_bo, L0_xattn_gn_w, L0_xattn_gn_b, L1_xattn_Wq, L1_xattn_Aq, L1_xattn_Bq, L1_xattn_Wk, L1_xattn_Ak, L1_xattn_Bk, L1_xattn_Wv, L1_xattn_Av, L1_xattn_Bv, L1_xattn_Wo, L1_xattn_Ao, L1_xattn_Bo):
    import jax
    import jax.numpy as jnp

    def _L0_xattn_ref(x, y, Wq, bq, Wk, bk, Wv, bv, Wo, bo, gn_w, gn_b):
        import jax, jax.numpy as jnp
        import numpy as np
        NUM_HEADS = 8
        EPS = 1e-05

        def _conv1x1(W, b, t):
            return jnp.einsum('oc,bcl->bol', W, t) + b[None, :, None]
        B, E, Lx = x.shape
        H = NUM_HEADS
        Dh = E // H
        q = _conv1x1(Wq, bq, y).reshape(B, H, Dh, -1)
        k = _conv1x1(Wk, bk, y).reshape(B, H, Dh, -1)
        v = _conv1x1(Wv, bv, x).reshape(B, H, Dh, Lx)
        scores = jnp.einsum('bhdl,bhel->bhde', q, k) / jnp.sqrt(jnp.float32(E))
        attn = jax.nn.softmax(scores, axis=-1)
        out = jnp.einsum('bhde,bhel->bhdl', attn, v).reshape(B, E, Lx)
        o = _conv1x1(Wo, bo, out) + x
        mu = jnp.mean(o, axis=(1, 2), keepdims=True)
        var = jnp.var(o, axis=(1, 2), keepdims=True)
        o_hat = (o - mu) * jax.lax.rsqrt(var + EPS)
        return o_hat * gn_w[None, :, None] + gn_b[None, :, None]

    def _L1_xattn_ref(hidden_states, traces, Wq, Aq, Bq, Wk, Ak, Bk, Wv, Av, Bv, Wo, Ao, Bo):
        import jax, jax.numpy as jnp
        import numpy as np
        H = 1024
        NH = 32
        NKV = 8
        HD = H // NH
        R = 16
        SCALING = 32.0 / 16.0

        def _lora_linear(x, W, A, B):
            return x @ W + SCALING * (x @ A @ B)
        bsz, q_len, _ = hidden_states.shape
        t_len = traces.shape[1]
        groups = NH // NKV
        q = _lora_linear(hidden_states, Wq, Aq, Bq).reshape(bsz, q_len, NH, HD)
        q = jnp.transpose(q, (0, 2, 1, 3))
        k = _lora_linear(traces, Wk, Ak, Bk).reshape(bsz, t_len, NKV, HD)
        v = _lora_linear(traces, Wv, Av, Bv).reshape(bsz, t_len, NKV, HD)
        k = jnp.transpose(k, (0, 2, 1, 3))
        v = jnp.transpose(v, (0, 2, 1, 3))
        k = jnp.repeat(k, groups, axis=1)
        v = jnp.repeat(v, groups, axis=1)
        scores = jnp.einsum('bhqd,bhtd->bhqt', q, k) / jnp.sqrt(jnp.asarray(HD, q.dtype))
        attn = jax.nn.softmax(scores, axis=-1)
        context = jnp.einsum('bhqt,bhtd->bhqd', attn, v)
        context = jnp.transpose(context, (0, 2, 1, 3)).reshape(bsz, q_len, H)
        out = _lora_linear(context, Wo, Ao, Bo)
        return hidden_states + out
    x = _L0_xattn_ref(x, ctx_4096, L0_xattn_Wq, L0_xattn_bq, L0_xattn_Wk, L0_xattn_bk, L0_xattn_Wv, L0_xattn_bv, L0_xattn_Wo, L0_xattn_bo, L0_xattn_gn_w, L0_xattn_gn_b)
    x = _L1_xattn_ref(x, ctx_4096, L1_xattn_Wq, L1_xattn_Aq, L1_xattn_Bq, L1_xattn_Wk, L1_xattn_Ak, L1_xattn_Bk, L1_xattn_Wv, L1_xattn_Av, L1_xattn_Bv, L1_xattn_Wo, L1_xattn_Ao, L1_xattn_Bo)
    return x

_drawn_inputs = setup_inputs


def setup_inputs(seed=0):
    import zlib

    import numpy as np

    out = dict(_drawn_inputs(seed))
    spreads = {'L0_xattn_bq': (0.0, 0.588),
     'L0_xattn_bk': (0.0, 0.587),
     'L0_xattn_bv': (0.0, 0.692),
     'L0_xattn_bo': (0.0, 0.1),
     'L0_xattn_gn_w': (1.0, 0.2),
     'L0_xattn_gn_b': (0.0, 0.1)}
    factors = {'L0_xattn_Wq': 2.965,
     'L0_xattn_Wk': 2.782,
     'L1_xattn_Aq': 8.0,
     'L1_xattn_Bq': 8.0,
     'L1_xattn_Ak': 8.0,
     'L1_xattn_Bk': 8.0}
    for name, (base, spread) in spreads.items():
        noise = np.random.default_rng([zlib.crc32(name.encode()), seed]).standard_normal(out[name].shape)
        drawn = base * np.exp(spread * noise) if base else spread * noise
        out[name] = jnp.asarray(drawn.astype(out[name].dtype))
    for name, factor in factors.items():
        out[name] = (out[name] * factor).astype(out[name].dtype)
    return out
```

```python
from contextlib import ExitStack

import concourse.bass as bass
from concourse import mybir

F32 = mybir.dt.float32
F32R = mybir.dt.float32r
ALU = mybir.AluOpType
ACT = mybir.ActivationFunctionType
AX_X = mybir.AxisListType.X

P = 128
BANK = 512
DMA = 16


class Signal:

    def __init__(self, sem):
        self.sem, self.count = sem, 0

    def mark(self, step):
        self.count += step
        return self, self.count


class Lane:

    def __init__(self):
        self.steps, self.passed = [], {}

    def wait(self, *marks):
        for signal, count in (m for m in marks if m is not None):
            if self.passed.get(signal, 0) < count:
                self.passed[signal] = count
                self.steps.append(lambda eng, s=signal.sem, c=count: eng.wait_ge(s, c))

    def do(self, make, signal=None, step=1):
        if signal is None:
            self.steps.append(make)
            return None
        self.steps.append(lambda eng, s=signal.sem: make(eng).then_inc(s, step))
        return signal.mark(step)

    def play(self, eng):
        for step in self.steps:
            step(eng)


def xattn_two_layers(nc, x, ctx_4096, Wq0, bq0, Wk0, bk0, Wv0, bv0, Wo0, bo0, gn_w, gn_b,
                     Wq, Aq, Bq, Wk, Ak, Bk, Wv, Av, Bv, Wo, Ao, Bo, out):
    B, E, L = x.shape
    HID = Wq.shape[1]
    KV = Wk.shape[1]
    R = Aq.shape[1]
    NC = HID // P
    HALF = HID // 2
    H0, D0 = 8, E // 8
    NH, HD = 32, HID // 32
    NKV = KV // HD
    GROUP = NH // NKV
    GQ = P // HD
    NQ = NKV // GQ
    UNITS = NQ * GROUP
    LORA_SCALE = 32.0 / 16.0
    SCORE0 = float(E) ** -0.5
    SCORE1 = float(HD) ** -0.5
    EPS = 1e-5
    OFF_BLOCK = -1e30
    assert E == P and HALF == BANK and 2 * KV == BANK and GQ * P == BANK and L == HID

    with ExitStack() as ctx:
        end = nc.sbuf_usable_end
        start = (nc.sbuf_base + 63) // 64 * 64
        at = [start]

        def sb(name, shape, dt=F32):
            size = 4
            for n in shape[1:]:
                size *= n
            a = at[0]
            at[0] = a + (size + 31) // 32 * 32
            assert at[0] <= end, (name, at[0], end)
            return nc.alloc_sbuf_tensor_at(name, shape, dt, offset=a)

        def signal(name):
            return Signal(ctx.enter_context(nc.semaphore(name)))

        def scratch(name, shape, dt=F32):
            return nc.dram_tensor(name, shape, dt, kind="Internal").ap()

        pe, act, dve, pool, sp = Lane(), Lane(), Lane(), Lane(), Lane()

        h_dram = scratch("h_dram", (B, P, HID))
        kT_dram = scratch("kT_dram", (B, P, KV // P * P))
        v_dram = scratch("v_dram", (B, P, KV))
        wo_dram = [scratch(f"wo_{s}_dram", (NC, P, HID)) for s in ("hi", "lo")]

        ident = sb("ident", [P, P])
        wq_hi = sb("wq_hi", [P, NC, HID], F32R)
        wq_lo = sb("wq_lo", [P, NC, HID], F32R)
        shared = at[0]

        wkv_hi = sb("wkv_hi", [P, NC, 2 * KV], F32R)
        wkv_lo = sb("wkv_lo", [P, NC, 2 * KV], F32R)
        y_in = [sb(f"y_in{i}", [P, L]) for i in range(2)]
        x_in = [sb(f"x_in{i}", [P, L]) for i in range(2)]
        yT = sb("yT", [P, NC, 2, P], F32R)
        x_hi = sb("x_hi", [P, L], F32R)
        x_lo = sb("x_lo", [P, L], F32R)
        h_out = [sb(f"h_out{i}", [P, L]) for i in range(2)]
        kv_sb = [sb(f"kv_sb{i}", [P, 2 * KV]) for i in range(2)]
        kT_sb = [sb(f"kT_sb{i}", [P, KV]) for i in range(2)]
        w_raw = [sb(f"w_raw{i}", [P, BANK]) for i in range(2)]
        o_split = [sb(f"o_split{i}", [P, 2, BANK], F32R) for i in range(2)]
        lora_aT = {m: sb(f"lora_aT_{m}", [P, HID], F32R) for m in ("kv", "q", "o")}
        lora_b = {m: sb(f"lora_b_{m}", [P, n], F32R) for m, n in (("kv", 2 * KV), ("q", HID), ("o", HID))}
        lora_raw = sb("lora_raw", [P, HID])
        lora_a = sb("lora_a", [P, NC, 2 * R])
        lora_a3 = h_out[0][:].rearrange("p (c n) -> p c n", c=NC)
        ones_avg = sb("ones_avg", [P, P])
        w0T = sb("w0T", [P, 3, P])
        wv0 = sb("wv0", [P, P])
        bias_rows = sb("bias_rows", [1, 2, P])
        ones_row = sb("ones_row", [1, P])
        bqk = sb("bqk", [P, 2, P])
        score_bias = sb("score_bias", [P, P])
        columns = sb("columns", [P, 5])
        bq_col, bv_col, bo_col, gnw_col, gnb_col = (columns[:, i:i + 1] for i in range(5))
        bq_scaled = sb("bq_scaled", [P, 1])
        minus_half = sb("minus_half", [P, 1])
        gram_right = sb("gram_right", [P, P])
        gram = sb("gram", [P, P])
        t1 = sb("t1", [P, P])
        s_bq = sb("s_bq", [P, P])
        att = sb("att", [P, P])
        n1 = sb("n1", [P, P])
        mix = sb("mix", [P, P])
        mix_split = sb("mix_split", [P, 2, P], F32R)
        y_sum = sb("y_sum", [P, 2])
        att_stat = sb("att_stat", [P, 4])
        norm = sb("norm", [P, 16])
        bn = sb("bn", [P, 2, 6])
        print_a = at[0]

        at[0] = shared
        wo_hi = sb("wo_hi", [P, NC, HID], F32R)
        wo_lo = sb("wo_lo", [P, NC, HID], F32R)
        h_early = sb("h_early", [P, HID])
        h_res = [sb(f"h_res{i}", [P, HID]) for i in range(2)]
        hT = sb("hT", [P, 2, NC, P], F32R)
        q_sb = sb("q_sb", [P, HID])
        qT = sb("qT", [P, 2, UNITS, P], F32R)
        k_in = sb("k_in", [P, NQ, P])
        v_in = sb("v_in", [P, NQ, GQ, HD])
        k_diag = sb("k_diag", [P, 2, NQ, GQ, P], F32R)
        v_pad = sb("v_pad", [P, 2, NQ, GQ, P], F32R)
        prob = [sb(f"prob{i}", [P, GQ, P]) for i in range(2)]
        probT = [sb(f"probT{i}", [P, 2, 2, GQ, P], F32R) for i in range(2)]
        cT = sb("cT", [P, 2, UNITS, P], F32R)
        soft = [sb(f"soft{i}", [P, 4, GQ]) for i in range(2)]

        banks = [ctx.enter_context(nc.psum_tensor(f"bank{i}", [P, 2 * BANK], F32)) for i in range(4)]

        def bank(i):
            return banks[i // 2][:, i % 2 * BANK:(i % 2 + 1) * BANK]

        def f32(ap):
            return ap.bitcast(F32)

        s_const = signal("s_const")
        s_pool = signal("s_pool")
        s_pe0 = signal("s_pe0")
        s_act0 = signal("s_act0")
        s_dve0 = signal("s_dve0")

        ident_zero = pool.do(lambda e: e.memset(ident[:], 0.0), s_pool)
        mask_zero = pool.do(lambda e: e.memset(score_bias[:], 0.0), s_pool)
        pool.wait(ident_zero)
        ident_ok = pool.do(lambda e: e.affine_select(
            out=ident[:], in_=ident[:], compare_op=ALU.not_equal, fill=1.0, base=0,
            pattern=[[-1, P]], channel_multiplier=1), s_pool)
        mask = score_bias[:].rearrange("p (b e) -> p b e", b=H0)
        pool.wait(mask_zero)
        above = pool.do(lambda e: e.affine_select(
            out=mask, in_=mask, compare_op=ALU.is_ge, fill=OFF_BLOCK, base=0,
            pattern=[[-D0, H0], [0, D0]], channel_multiplier=1), s_pool)
        pool.wait(above)
        mask_ok = pool.do(lambda e: e.affine_select(
            out=mask, in_=mask, compare_op=ALU.is_ge, fill=OFF_BLOCK, base=D0 - 1,
            pattern=[[D0, H0], [0, D0]], channel_multiplier=-1), s_pool)
        ones_ok = pool.do(lambda e: e.memset(ones_row[:], 1.0), s_pool)
        pool.do(lambda e: e.memset(minus_half[:], -0.5), s_pool)
        avg_ok = pool.do(lambda e: e.memset(ones_avg[:], 1.0 / P), s_pool)

        def load(dst, src, sig):
            return sp.do(lambda e: e.dma_start(dst, src), sig, DMA)

        s_y = [signal(f"s_y{i}") for i in range(2)]
        s_x = [signal(f"s_x{i}") for i in range(2)]
        s_wraw = [signal(f"s_wraw{i}") for i in range(2)]
        s_lora = signal("s_lora")
        s_w0 = signal("s_w0")

        def chunk_rows(w, permuted):
            if permuted:
                return w.rearrange("(q g j d) n -> q j g d n", q=NQ, g=GQ, j=GROUP)
            return w.rearrange("(c p) n -> c p n", p=P)

        def chunk_of(w, c, permuted):
            rows = chunk_rows(w, permuted)
            return rows[c // GROUP, c % GROUP] if permuted else rows[c]

        def to_partitions(tile_ap, permuted):
            return tile_ap.rearrange("(g d) n -> g d n", g=GQ) if permuted else tile_ap

        raw0 = None
        y_loaded = {0: load(y_in[0][:], ctx_4096[0], s_y[0])}
        w0_tmp = [x_in[1][:, i * P:(i + 1) * P] for i in range(3)]
        for dst, src in ((w0_tmp[0], Wq0), (w0_tmp[1], Wk0), (w0_tmp[2], Wo0), (wv0[:], Wv0)):
            load(dst, src, s_w0)
        for row, src in ((0, bq0), (1, bk0)):
            load(bias_rows[:, row, :], src.rearrange("(a n) -> a n", a=1), s_w0)
        for col, src in ((bq_col, bq0), (bv_col, bv0), (bo_col, bo0), (gnw_col, gn_w), (gnb_col, gn_b)):
            w0_loaded = load(col, src.rearrange("(n a) -> n a", a=1), s_w0)

        factors = {"kv": ((Ak, 0, Bk, 0), (Av, R, Bv, KV)), "q": ((Aq, 0, Bq, 0),), "o": ((Ao, 0, Bo, 0),)}
        lora_done = None
        lora_ready = {}
        tr_free = {0: None, 1: None}
        for m, parts in factors.items():
            n_cols = lora_b[m].shape[1]
            a_cleared = dve_clear = None
            dve.wait(lora_done)
            dve.do(lambda e: e.memset(lora_a3, 0.0))
            cleared = dve.do(lambda e: e.memset(lora_raw[:], 0.0), s_dve0)
            sp.wait(cleared)
            for a, first, b, col in parts:
                for c in range(NC):
                    for g in range(GQ if m == "o" else 1):
                        rows = chunk_of(a, c, m == "o")
                        if m == "o":
                            dst = lora_a[g * HD:(g + 1) * HD, c, first:first + R]
                            rows = rows[g]
                        else:
                            dst = lora_a[:, c, first:first + R]
                        if m == "o" or c == 0:
                            if m != "o":
                                dst = lora_a[:, :, first:first + R]
                                rows = a.rearrange("(c p) r -> p c r", p=P)
                            load(dst, rows, s_lora)
                for q in range(3):
                    loaded = load(lora_raw[32 * q + first:32 * q + first + R, col:col + b.shape[1]], b, s_lora)
            used = R * len(parts)
            dve.wait(loaded)
            for q in range(3):
                a3_ok = dve.do(lambda e, q=q, used=used: e.tensor_copy(
                    lora_a3[:, :, 32 * q:32 * q + used], lora_a[:, :, 0:used]), s_dve0)
            dve.do(lambda e, m=m, n=n_cols: e.tensor_copy(lora_b[m][:], lora_raw[:, 0:n]), s_dve0)
            dve.wait((s_dve0, s_dve0.count))
            b_ok = dve.do(lambda e, m=m, n=n_cols: e.tensor_tensor(
                lora_b[m][64:96, :], lora_raw[64:96, 0:n], f32(lora_b[m][64:96, :]), ALU.subtract), s_dve0)
            pe.wait(a3_ok, ident_ok)
            for half in range(2):
                pe.wait(tr_free[half])
                for c in range(4):
                    turned = pe.do(lambda e, half=half, c=c: e.transpose(
                        bank(4 + half)[:, c * P:(c + 1) * P], lora_a3[:, 4 * half + c, :], ident[:]), s_pe0)
                dst = lora_aT[m][:, half * BANK:(half + 1) * BANK]
                dve.wait(turned)
                hi = dve.do(lambda e, dst=dst, half=half: e.tensor_copy(dst, bank(4 + half)), s_dve0)
                dve.wait(hi)
                tr_free[half] = lora_done = dve.do(lambda e, dst=dst, half=half: e.tensor_tensor(
                    dst[32:64, :], bank(4 + half)[32:64, :], f32(dst[32:64, :]), ALU.subtract), s_dve0)
            lora_ready[m] = lora_done

        pe.wait(w0_loaded, ident_ok, ones_ok)
        for i in range(3):
            turned = pe.do(lambda e, i=i: e.transpose(bank(3)[:, i * P:(i + 1) * P], w0_tmp[i], ident[:]), s_pe0)
        act.wait(turned)
        w0T_ok = act.do(lambda e: e.copy(w0T[:].rearrange("p a b -> p (a b)"), bank(3)[:, 0:3 * P]), s_act0)
        pe.wait(w0T_ok)
        for i in range(2):
            spread = pe.do(lambda e, i=i: e.matmul(bank(3)[:, i * P:(i + 1) * P], ones_row[:],
                                                   bias_rows[:, i, :], start=True, stop=True), s_pe0)
        act.wait(spread)
        bqk_ok = act.do(lambda e: e.copy(bqk[:].rearrange("p a b -> p (a b)"), bank(3)[:, 0:2 * P]), s_act0)
        wqT0, wkT0, woT0 = (w0T[:, i, :] for i in range(3))
        dve.wait(bqk_ok, mask_ok)
        scaled = dve.do(lambda e: e.tensor_scalar(bq_scaled[:], bq_col, SCORE0 * L, None, ALU.mult), s_dve0)
        dve.wait(scaled, w0_loaded)
        score_bias_ok = dve.do(lambda e: e.scalar_tensor_tensor(
            score_bias[:], bqk[:, 1, :], bq_scaled[:], score_bias[:], ALU.mult, ALU.add), s_dve0)

        small_free = [None, None]
        small_turn = [0]

        def small_bank():
            i = small_turn[0] % 2
            small_turn[0] += 1
            pe.wait(small_free[i])
            return i, bank(6 + i)

        s_prep = signal("s_prep")
        s_prep_w = signal("s_prep_w")
        s_prep_hi = signal("s_prep_hi")
        s_prep_lo = signal("s_prep_lo")
        s_wo_out = [signal(f"s_wo_out{i}") for i in range(2)]
        raw_free = [None, None]
        raw_loaded = {}
        o_stored = [None, None]
        units = [("kv", c, 0) for c in range(NC)]
        units += [(m, c, half) for m in ("q", "o") for c in range(NC) for half in range(2)]

        def load_raw(n):
            if n >= len(units):
                return
            m, c, half = units[n]
            i = n % 2
            sp.wait(raw_free[i])
            if m == "kv":
                load(w_raw[i][:, 0:KV], chunk_of(Wk, c, False), s_wraw[i])
                raw_loaded[n] = load(w_raw[i][:, KV:2 * KV], chunk_of(Wv, c, False), s_wraw[i])
            elif m == "q":
                raw_loaded[n] = load(w_raw[i][:], chunk_of(Wq, c, False)[:, half * BANK:(half + 1) * BANK],
                                     s_wraw[i])
            else:
                rows = chunk_of(Wo, c, True)
                for g in range(GQ):
                    raw_loaded[n] = load(w_raw[i][g * HD:(g + 1) * HD, :],
                                         rows[g, :, half * BANK:(half + 1) * BANK], s_wraw[i])

        prep_at = {}

        def prep_product(n):
            m, c, half = units[n]
            i, ps = small_bank()
            pe.wait(lora_ready[m])
            prep_at[n] = i, pe.do(lambda e: e.matmul(
                ps, lora_aT[m][:, c * P:(c + 1) * P], lora_b[m][:, half * BANK:(half + 1) * BANK],
                start=True, stop=True), s_prep)

        def prep_merge(n):
            i, product = prep_at[n]
            raw = w_raw[n % 2][:]
            dve.wait(product, raw_loaded[n])
            small_free[i] = dve.do(lambda e: e.scalar_tensor_tensor(
                raw, bank(6 + i), LORA_SCALE, raw, ALU.mult, ALU.add), s_prep_w)
            return small_free[i]

        def prep_split(n, merged):
            m, c, half = units[n]
            raw = w_raw[n % 2][:]
            if m == "kv":
                hi, lo = wkv_hi[:, c, :], wkv_lo[:, c, :]
            elif m == "q":
                raw = raw.rearrange("p (g j d) -> p g j d", g=GQ, j=GROUP)
                hi, lo = (w[:, c, half * BANK:(half + 1) * BANK].rearrange(
                    "p (j g d) -> p g j d", g=GQ, j=GROUP) for w in (wq_hi, wq_lo))
            else:
                hi, lo = o_split[n % 2][:, 0, :], o_split[n % 2][:, 1, :]
                act.wait(o_stored[n % 2])
            act.wait(merged)
            hi_ok = act.do(lambda e: e.copy(hi, raw), s_prep_hi)
            dve.wait(hi_ok)
            lo_ok = dve.do(lambda e: e.tensor_tensor(lo, raw, f32(hi), ALU.subtract), s_prep_lo)
            raw_free[n % 2] = lo_ok
            if m == "o":
                sp.wait(lo_ok)
                for part in range(2):
                    o_stored[n % 2] = sp.do(lambda e, part=part: e.dma_start(
                        wo_dram[part][c, :, half * BANK:(half + 1) * BANK], f32(o_split[n % 2][:, part, :])),
                        s_wo_out[n % 2], DMA)
            return lo_ok

        load_raw(0)
        load_raw(1)
        for n in range(NC):
            prep_product(n)
            wkv_ok = prep_split(n, prep_merge(n))
            load_raw(n + 2)
        next_unit = [NC]

        names_a = ("yT_mm", "yT_hi", "yT_lo", "ysum", "gram_mm", "gram_r", "gram", "t1_mm", "t1", "sbq",
                   "s_mm", "s_sb", "s_max", "s_neg", "s_exp", "s_rec", "att", "n1_mm", "n1", "mix_mm",
                   "mix", "mix_hi", "mix_lo", "xbias", "x_hi", "x_lo", "mx_mm", "bn", "agg", "st",
                   "st1_mm", "dev", "nm", "st2", "st2_mm", "ve", "pow", "gsc", "gbi", "h", "kv_mm",
                   "kv", "kT_mm", "kT")
        S = {n: signal("a_" + n) for n in names_a}
        s_h_out = [signal(f"s_h_out{i}") for i in range(2)]
        s_kv_out = [signal(f"s_kv_out{i}") for i in range(2)]
        M = {}

        def mark(stage, b):
            return M.get((stage, b))

        def load_y(b):
            if 0 < b < B:
                sp.wait(mark("yT_mm", b - 2), mark("ysum", b - 2))
                y_loaded[b] = load(y_in[b % 2][:], ctx_4096[b], s_y[b % 2])

        x_loaded = {}

        def load_x(b):
            if b < B:
                sp.wait(mark("x_hi", b - 2), mark("x_lo", b - 2))
                if b == 1:
                    sp.wait(w0T_ok)
                x_loaded[b] = load(x_in[b % 2][:], x[b], s_x[b % 2])

        def turn_y(b):
            pe.wait(y_loaded[b], ident_ok, mark("yT_hi", b - 1), mark("yT_lo", b - 1))
            for c in range(NC):
                m = pe.do(lambda e, c=c: e.transpose(
                    banks[0][:, c * P:(c + 1) * P], y_in[b % 2][:, c * P:(c + 1) * P], ident[:]),
                    S["yT_mm"] if c == NC - 1 else None)
            M["yT_mm", b] = m

        def split_yT(b):
            ps = banks[0][:].rearrange("p (c n) -> p c n", c=NC)
            act.wait(mark("yT_mm", b), mark("kv_mm", b - 1), mark("gram_mm", b - 1))
            M["yT_hi", b] = act.do(lambda e: e.copy(yT[:, :, 0, :], ps), S["yT_hi"])
            dve.wait(mark("yT_hi", b))
            M["yT_lo", b] = dve.do(lambda e: e.tensor_tensor(
                yT[:, :, 1, :], ps, f32(yT[:, :, 0, :]), ALU.subtract), S["yT_lo"])

        def sum_y(b):
            dve.wait(y_loaded[b], mark("t1", b - 2), mark("sbq", b - 2))
            M["ysum", b] = dve.do(lambda e: e.tensor_reduce(
                y_sum[:, b % 2:b % 2 + 1], y_in[b % 2][:], AX_X, ALU.add), S["ysum"])

        def kv_products(b, chunks):
            pe.wait(mark("yT_hi", b), mark("yT_lo", b), wkv_ok, mark("kv", b - 1))
            for c in chunks:
                for part, w in ((0, wkv_hi), (0, wkv_lo), (1, wkv_hi)):
                    first = c == 0 and part == 0 and w is wkv_hi
                    last = c == NC - 1 and part == 1
                    m = pe.do(lambda e, c=c, part=part, w=w, first=first, last=last: e.matmul(
                        bank(2), yT[:, c, part, :], w[:, c, :], start=first, stop=last),
                        S["kv_mm"] if last else None)
            M["kv_mm", b] = m

        def gram_products(b):
            pe.wait(mark("yT_hi", b), mark("yT_lo", b), mark("gram_r", b - 1), mark("gram", b - 1), w0T_ok, bqk_ok)
            for c in range(NC):
                for part in range(2):
                    last = c == NC - 1 and part == 1
                    m = pe.do(lambda e, c=c, part=part, last=last: e.matmul(
                        bank(3)[:, 0:2 * P], yT[:, c, part, :], yT[:, c, :, :],
                        start=c == 0 and part == 0, stop=last), S["gram_mm"] if last else None)
            M["gram_mm", b] = m

        def sum_gram(b):
            act.wait(mark("gram_mm", b), mark("gram", b - 1))
            M["gram_r", b] = act.do(lambda e: e.copy(gram_right[:], bank(3)[:, P:2 * P]), S["gram_r"])
            dve.wait(mark("gram_r", b), mark("t1_mm", b - 1))
            M["gram", b] = dve.do(lambda e: e.tensor_tensor(
                gram[:], bank(3)[:, 0:P], gram_right[:], ALU.add), S["gram"])

        def small_product(stage, b, lhsT, rhs, *waits):
            i, ps = small_bank()
            pe.wait(*waits)
            M[stage, b] = pe.do(lambda e: e.matmul(ps[:, 0:rhs.shape[1]], lhsT, rhs, start=True, stop=True),
                                S[stage])
            return i

        held = {}

        def t1_product(b):
            held["t1", b] = small_product("t1_mm", b, gram[:], wkT0, mark("gram", b))

        def evacuate_t1(b):
            i = held["t1", b]
            s = y_sum[:, b % 2:b % 2 + 1]
            dve.wait(mark("t1_mm", b), mark("ysum", b), mark("s_mm", b - 1), bqk_ok)
            small_free[i] = M["t1", b] = dve.do(lambda e: e.scalar_tensor_tensor(
                t1[:], bqk[:, 1, :], s, bank(6 + i)[:, 0:P], ALU.mult, ALU.add), S["t1"])
            M["sbq", b] = dve.do(lambda e: e.tensor_scalar(s_bq[:], bqk[:, 0, :], s, None, ALU.mult), S["sbq"])

        def score_product(b):
            i, ps = small_bank()
            pe.wait(mark("t1", b), mark("sbq", b))
            pe.do(lambda e: e.matmul(ps[:, 0:P], wqT0, t1[:], start=True, stop=False))
            M["s_mm", b] = pe.do(lambda e: e.matmul(ps[:, 0:P], s_bq[:], wkT0, start=False, stop=True), S["s_mm"])
            held["s", b] = i

        def softmax0_begin(b):
            i = held["s", b]
            dve.wait(mark("s_mm", b), score_bias_ok, mark("n1_mm", b - 1))
            small_free[i] = dve.do(lambda e: e.scalar_tensor_tensor(
                att[:], bank(6 + i)[:, 0:P], SCORE0, score_bias[:], ALU.mult, ALU.add), S["s_sb"])
            dve.wait(small_free[i])
            top = dve.do(lambda e: e.tensor_reduce(att_stat[:, 0:1], att[:], AX_X, ALU.max), S["s_max"])
            dve.wait(top)
            neg = dve.do(lambda e: e.tensor_scalar(att_stat[:, 1:2], att_stat[:, 0:1], -1.0, None, ALU.mult),
                         S["s_neg"])
            act.wait(neg)
            M["s_exp", b] = act.do(lambda e: e.activation(
                att[:], att[:], ACT.Exp, bias=att_stat[:, 1:2], scale=1.0, accum_out=att_stat[:, 2:3]),
                S["s_exp"])

        def softmax0_end(b):
            dve.wait(mark("s_exp", b))
            inverse = dve.do(lambda e: e.reciprocal(att_stat[:, 3:4], att_stat[:, 2:3]), S["s_rec"])
            dve.wait(inverse)
            M["att", b] = dve.do(lambda e: e.tensor_scalar(att[:], att[:], att_stat[:, 3:4], None, ALU.mult),
                                 S["att"])

        def n1_product(b):
            held["n1", b] = small_product("n1_mm", b, att[:], woT0, mark("att", b))

        def evacuate_n1(b):
            i = held["n1", b]
            act.wait(mark("n1_mm", b), mark("mix_mm", b - 1))
            small_free[i] = M["n1", b] = act.do(lambda e: e.copy(n1[:], bank(6 + i)[:, 0:P]), S["n1"])

        def mix_product(b):
            i, ps = small_bank()
            pe.wait(mark("n1", b))
            pe.do(lambda e: e.matmul(ps[:, 0:P], wv0[:], n1[:], start=True, stop=True))
            M["mix_mm", b] = pe.do(lambda e: e.matmul(ps[:, P:P + 1], n1[:], bv_col, start=True, stop=True),
                                   S["mix_mm"])
            held["mix", b] = i

        xbias, mv, st, dev, nm, st2, ve, rstd, gsc, gbi = (
            norm[:, 0:1], norm[:, 1:3], norm[:, 3:4], norm[:, 4:5], norm[:, 5:6], norm[:, 6:7],
            norm[:, 7:8], norm[:, 8:9], norm[:, 9:10], norm[:, 10:11])

        def split_mix(b):
            i = held["mix", b]
            dve.wait(mark("mix_mm", b), mark("mx_mm", b - 1))
            M["mix", b] = dve.do(lambda e: e.tensor_tensor(mix[:], bank(6 + i)[:, 0:P], ident[:], ALU.add), S["mix"])
            small_free[i] = M["xbias", b] = dve.do(lambda e: e.tensor_tensor(
                xbias, bank(6 + i)[:, P:P + 1], bo_col, ALU.add), S["xbias"])
            dve.wait(mark("mix", b))
            M["mix_hi", b] = dve.do(lambda e: e.tensor_copy(mix_split[:, 0, :], mix[:]), S["mix_hi"])
            dve.wait(mark("mix_hi", b))
            M["mix_lo", b] = dve.do(lambda e: e.tensor_tensor(
                mix_split[:, 1, :], mix[:], f32(mix_split[:, 0, :]), ALU.subtract), S["mix_lo"])

        def split_x(b):
            if not 0 <= b < B:
                return
            act.wait(x_loaded[b], mark("mx_mm", b - 1))
            M["x_hi", b] = act.do(lambda e: e.copy(x_hi[:], x_in[b % 2][:]), S["x_hi"])
            dve.wait(mark("x_hi", b))
            M["x_lo", b] = dve.do(lambda e: e.tensor_tensor(x_lo[:], x_in[b % 2][:], f32(x_hi[:]), ALU.subtract),
                                  S["x_lo"])

        def mixed_x(b):
            pe.wait(mark("mix_lo", b), mark("x_lo", b), mark("h", b - 1), tr_free[0], tr_free[1])
            for part, xs in ((0, x_hi), (0, x_lo), (1, x_hi)):
                for half in range(2):
                    first, last = part == 0 and xs is x_hi, part == 1
                    m = pe.do(lambda e, part=part, xs=xs, half=half, first=first, last=last: e.matmul(
                        bank(4 + half), mix_split[:, part, :], xs[:, half * BANK:(half + 1) * BANK],
                        start=first, stop=last), S["mx_mm"] if last and half else None)
            M["mx_mm", b] = m

        def partition_stats(b):
            dve.wait(mark("mx_mm", b), mark("xbias", b))
            for half in range(2):
                m = dve.do(lambda e, half=half: e.bn_stats(bn[:, half, :], bank(4 + half)), S["bn"])
            dve.wait(m)
            m = dve.do(lambda e: e.bn_aggr(mv, bn[:].rearrange("p a b -> p (a b)")), S["agg"])
            dve.wait(m)
            M["st", b] = dve.do(lambda e: e.tensor_tensor(st, mv[:, 0:1], xbias, ALU.add), S["st"])

        def mean_product(b):
            held["st1", b] = small_product("st1_mm", b, ones_avg[:], st, mark("st", b), avg_ok)

        def deviation(b):
            i = held["st1", b]
            mean = bank(6 + i)[:, 0:1]
            dve.wait(mark("st1_mm", b))
            m = dve.do(lambda e: e.tensor_tensor(dev, st, mean, ALU.subtract), S["dev"])
            small_free[i] = M["nm", b] = dve.do(lambda e: e.tensor_tensor(nm, xbias, mean, ALU.subtract), S["nm"])
            dve.wait(m)
            M["st2", b] = dve.do(lambda e: e.scalar_tensor_tensor(st2, dev, dev, mv[:, 1:2], ALU.mult, ALU.add),
                                 S["st2"])

        def var_product(b):
            held["st2", b] = small_product("st2_mm", b, ones_avg[:], st2, mark("st2", b))

        def norm_factors(b):
            i = held["st2", b]
            dve.wait(mark("st2_mm", b), mark("h", b - 1))
            small_free[i] = m = dve.do(lambda e: e.tensor_scalar(ve, bank(6 + i)[:, 0:1], EPS, None, ALU.add), S["ve"])
            pool.wait(m)
            m = pool.do(lambda e: e.tensor_tensor(rstd, ve, minus_half[:], ALU.pow), S["pow"])
            dve.wait(m, w0_loaded)
            m = dve.do(lambda e: e.tensor_tensor(gsc, rstd, gnw_col, ALU.mult), S["gsc"])
            dve.wait(m, mark("nm", b))
            M["gbi", b] = dve.do(lambda e: e.scalar_tensor_tensor(gbi, nm, gsc, gnb_col, ALU.mult, ALU.add), S["gbi"])

        h_stored = {}
        kv_stored = {}

        def write_h(b):
            act.wait(mark("gbi", b), mark("mx_mm", b), h_stored.get(b - 2), lora_done)
            M["h", b] = act.do(lambda e: e.activation(
                h_out[b % 2][:], banks[2][:], ACT.Identity, bias=gbi, scale=gsc), S["h"])
            sp.wait(mark("h", b))
            h_stored[b] = sp.do(lambda e: e.dma_start(h_dram[b], h_out[b % 2][:]), s_h_out[b % 2], DMA)

        def evacuate_kv(b):
            act.wait(mark("kv_mm", b), kv_stored.get(b - 2), mark("kT_mm", b - 2))
            M["kv", b] = act.do(lambda e: e.copy(kv_sb[b % 2][:], bank(2)), S["kv"])

        def turn_k(b):
            i, ps = small_bank()
            pe.wait(mark("kv", b))
            for c in range(KV // P):
                m = pe.do(lambda e, c=c: e.transpose(
                    ps[:, c * P:(c + 1) * P], kv_sb[b % 2][:, c * P:(c + 1) * P], ident[:]),
                    S["kT_mm"] if c == KV // P - 1 else None)
            M["kT_mm", b] = m
            held["kT", b] = i

        def evacuate_kT(b):
            i = held["kT", b]
            act.wait(mark("kT_mm", b), kv_stored.get(b - 2))
            small_free[i] = M["kT", b] = act.do(lambda e: e.copy(kT_sb[b % 2][:], bank(6 + i)[:, 0:KV]), S["kT"])
            sp.wait(mark("kv", b), mark("kT", b))
            sp.do(lambda e: e.dma_start(v_dram[b], kv_sb[b % 2][:, KV:2 * KV]), s_kv_out[b % 2], DMA)
            kv_stored[b] = sp.do(lambda e: e.dma_start(kT_dram[b], kT_sb[b % 2][:]), s_kv_out[b % 2], DMA)

        load_y(1)
        load_x(0)
        load_x(1)
        turn_y(0)
        split_yT(0)
        sum_y(0)
        for i in range(B + 2):
            cur, prev, old, nxt = i < B, 0 <= i - 1 < B, 0 <= i - 2 < B, i + 1 < B
            unit = next_unit[0] if next_unit[0] < len(units) and cur else None
            if prev:
                t1_product(i - 1)
                evacuate_t1(i - 1)
            if old:
                mix_product(i - 2)
                split_mix(i - 2)
            if cur:
                kv_products(i, range(NC // 2))
            if prev:
                score_product(i - 1)
                softmax0_begin(i - 1)
            if old:
                mixed_x(i - 2)
                partition_stats(i - 2)
            if prev:
                softmax0_end(i - 1)
            if cur:
                gram_products(i)
                sum_gram(i)
            if old:
                mean_product(i - 2)
                deviation(i - 2)
            if unit is not None:
                prep_product(unit)
                merged = prep_merge(unit)
            if cur:
                kv_products(i, range(NC // 2, NC))
                evacuate_kv(i)
            if old:
                var_product(i - 2)
                norm_factors(i - 2)
            if prev:
                n1_product(i - 1)
                evacuate_n1(i - 1)
            if nxt:
                turn_y(i + 1)
                split_yT(i + 1)
                sum_y(i + 1)
            if old:
                write_h(i - 2)
            if cur:
                turn_k(i)
                evacuate_kT(i)
            split_x(i - 1)
            if unit is not None:
                prep_split(unit, merged)
                load_raw(unit + 2)
                next_unit[0] += 1
            load_y(i + 2)
            load_x(i + 1 if i else B)
        assert next_unit[0] == len(units)

        s_end = {n: signal(f"s_end_{n}") for n in ("pe", "act", "dve", "pool")}
        phase_a = [mark("kT_mm", B - 1), mark("n1_mm", B - 1), mark("mx_mm", B - 1), mark("st2_mm", B - 1),
                   mark("kT", B - 1), mark("h", B - 1), mark("gbi", B - 1), mark("x_lo", B - 1),
                   (s_prep_lo, s_prep_lo.count), (s_prep_hi, s_prep_hi.count), mark("sbq", B - 1)]
        stored = [h_stored[B - 2], h_stored[B - 1], kv_stored[B - 2], kv_stored[B - 1], *o_stored]
        sp.wait(*phase_a, *stored)

        s_wo_in = signal("s_wo_in")
        s_he = signal("s_he")
        s_hr = [signal(f"s_hr{i}") for i in range(2)]
        s_k = signal("s_k")
        s_v = signal("s_v")
        s_out = [signal(f"s_out{i}") for i in range(2)]
        names_b = ("kd", "vp", "hT_mm", "hT_hi", "hT_lo", "q_mm", "q", "qT_mm", "qT_hi", "qT_lo", "sc_mm",
                   "max", "neg", "exp", "rec", "norm", "pT_mm", "pT_hi", "pT_lo", "pv_mm", "c_hi", "c_lo",
                   "o_mm", "o")
        S.update({n: signal("b_" + n) for n in names_b})

        pool.wait(*phase_a, *stored)
        pool.do(lambda e: e.memset(k_diag[:].bitcast(F32), 0.0))
        pads_ok = pool.do(lambda e: e.memset(v_pad[:].bitcast(F32), 0.0), s_pool)
        pool.wait(pads_ok)

        def in_range(b):
            return 0 <= b < B

        def load_h_early(b):
            if in_range(b):
                sp.wait(mark("hT_mm", (b - 1, 1)))
                M["h_early", b] = load(h_early[:], h_dram[b], s_he)

        def load_k(b):
            if in_range(b):
                sp.wait(mark("kd", (b - 1, NQ - 1)))
                M["k_in", b] = load(k_in[:], kT_dram[b].rearrange("p (q t) -> p q t", q=NQ), s_k)

        def load_v(b):
            if in_range(b):
                sp.wait(mark("vp", (b - 1, NQ - 1)))
                M["v_in", b] = load(v_in[:], v_dram[b].rearrange("p (q g d) -> p q g d", q=NQ, g=GQ), s_v)

        def load_h_res(b):
            if in_range(b):
                sp.wait(mark("out", b - 2))
                M["h_res", b] = load(h_res[b % 2][:], h_dram[b], s_hr[b % 2])

        def after_pool(*marks):
            pool.wait(M.get("pool"), *marks)

        def keys_diagonal(b, q):
            if not in_range(b):
                return
            pool.wait(M["k_in", b], mark("sc_mm", (b - 1) * UNITS + (q + 1) * GROUP - 1))
            for g in range(GQ):
                rows = slice(g * HD, (g + 1) * HD)
                after_pool()
                M["pool"] = pool.do(lambda e, rows=rows, g=g: e.tensor_scalar(
                    k_diag[rows, 0, q, g, :], k_in[rows, q, :], 1.0, None, ALU.mult), S["kd"])
                after_pool()
                M["pool"] = pool.do(lambda e, rows=rows, g=g: e.tensor_tensor(
                    k_diag[rows, 1, q, g, :], k_in[rows, q, :], f32(k_diag[rows, 0, q, g, :]), ALU.subtract),
                    S["kd"])
            M["kd", (b, q)] = M["pool"]

        def padded(part, q):
            return v_pad[:, part, q, :, :].rearrange("p g (r d) -> p (g r) d", r=GQ)[:, 0:GQ * GQ:GQ + 1, :]

        def values_padded(b, q):
            if not in_range(b):
                return
            after_pool(M["v_in", b], mark("pv_mm", ((b - 1) * NQ + q) * 2 + 1))
            m = pool.do(lambda e: e.tensor_scalar(padded(0, q), v_in[:, q, :, :], 1.0, None, ALU.mult), S["vp"])
            pool.wait(m)
            M["pool"] = M["vp", (b, q)] = pool.do(lambda e: e.tensor_tensor(
                padded(1, q), v_in[:, q, :, :], f32(padded(0, q)), ALU.subtract), S["vp"])

        TURN = bank(7)

        def split_turned(stage, b, half, dst, *waits):
            act.wait(mark(stage + "_mm", (b, half)), *waits)
            M[stage + "_hi", (b, half)] = act.do(lambda e: e.copy(dst(0), TURN), S[stage + "_hi"])
            dve.wait(mark(stage + "_hi", (b, half)))
            M[stage + "_lo", (b, half)] = dve.do(lambda e: e.tensor_tensor(
                dst(1), TURN, f32(dst(0)), ALU.subtract), S[stage + "_lo"])
            M["turned"] = M[stage + "_lo", (b, half)]

        def turn(stage, b, half, src, *waits):
            pe.wait(M.get("turned"), *waits)
            for c in range(4):
                m = pe.do(lambda e, c=c: e.transpose(TURN[:, c * P:(c + 1) * P], src(4 * half + c), ident[:]),
                          S[stage + "_mm"] if c == 3 else None)
            M[stage + "_mm", (b, half)] = m

        def turn_h(b, half):
            if in_range(b):
                turn("hT", b, half, lambda c: h_early[:, c * P:(c + 1) * P], M["h_early", b])

        def split_hT(b, half):
            if in_range(b):
                split_turned("hT", b, half, lambda part: hT[:, part, 4 * half:4 * half + 4, :].rearrange(
                    "p c n -> p (c n)"), mark("q_mm", b - 1))

        def turn_q(b, half):
            if in_range(b):
                turn("qT", b, half, lambda c: q_sb[:, c * P:(c + 1) * P], mark("q", b))

        def split_qT(b, half):
            if in_range(b):
                split_turned("qT", b, half, lambda part: qT[:, part, 4 * half:4 * half + 4, :].rearrange(
                    "p c n -> p (c n)"), mark("sc_mm", (b - 1) * UNITS + (half + 1) * GROUP - 1))

        def project(stage, b, left, weights, chunks):
            hi, lo = weights
            for c in chunks:
                for part, w in ((0, hi), (0, lo), (1, hi)):
                    for half in range(2):
                        first = c == 0 and part == 0 and w is hi
                        last = c == NC - 1 and part == 1
                        m = pe.do(lambda e, c=c, part=part, w=w, half=half, first=first, last=last: e.matmul(
                            bank(half), left[:, part, c, :], w[:, c, half * BANK:(half + 1) * BANK],
                            start=first, stop=last), S[stage] if half and part == 1 else None)
                M[stage, (b, c)] = m
            M[stage, b] = m

        def project_q(b, s):
            if in_range(b):
                pe.wait(mark("hT_lo", (b, 2 * s // 4)), mark("o", b - 3), (s_prep_lo, s_prep_lo.count))
                project("q_mm", b, hT, (wq_hi, wq_lo), range(2 * s, 2 * s + 2))

        def evacuate_q(b):
            if in_range(b):
                act.wait(mark("q_mm", b), mark("qT_mm", (b - 1, 1)))
                M["q", b] = act.do(lambda e: e.copy(q_sb[:], banks[0][:]), S["q"])

        def project_o(b, s):
            if in_range(b):
                pe.wait(mark("c_lo", (b, 2 * s // GROUP)), mark("q", b + 2), mark("o", b - 1), M["wo_in", s // 2])
                project("o_mm", b, cT, (wo_hi, wo_lo), range(2 * s, 2 * s + 2))

        def finish_out(b):
            if in_range(b):
                dve.wait(mark("o_mm", b), M["h_res", b])
                M["o", b] = dve.do(lambda e: e.tensor_tensor(
                    h_res[b % 2][:], banks[0][:], h_res[b % 2][:], ALU.add), S["o"])
                sp.wait(mark("o", b))
                M["out", b] = sp.do(lambda e: e.dma_start(out[b], h_res[b % 2][:]), s_out[b % 2], DMA)

        total = B * UNITS

        def scores(t):
            if not 0 <= t < total:
                return
            b, u = divmod(t, UNITS)
            q = u // GROUP
            pe.wait(mark("qT_lo", (b, q)), mark("kd", (b, q)), mark("exp", t - 2))
            for n, (part, kpart) in enumerate(((0, 0), (0, 1), (1, 0))):
                m = pe.do(lambda e, n=n, part=part, kpart=kpart: e.matmul(
                    bank(2 + t % 2), qT[:, part, u, :], k_diag[:, kpart, q, :, :].rearrange("p g t -> p (g t)"),
                    start=n == 0, stop=n == 2), S["sc_mm"] if n == 2 else None)
            M["sc_mm", t] = m

        def maxima(t):
            if not 0 <= t < total:
                return
            st_t = soft[t % 2]
            dve.wait(mark("sc_mm", t), mark("exp", t - 2))
            m = dve.do(lambda e: e.tensor_reduce(
                st_t[:, 0, :], bank(2 + t % 2).rearrange("p (g t) -> p g t", g=GQ), AX_X, ALU.max), S["max"])
            dve.wait(m)
            M["neg", t] = dve.do(lambda e: e.tensor_scalar(st_t[:, 1, :], st_t[:, 0, :], -SCORE1, None, ALU.mult),
                                 S["neg"])

        def exponents(t):
            if not 0 <= t < total:
                return
            st_t = soft[t % 2]
            act.wait(mark("neg", t), mark("pT_mm", t - 2), mark("norm", t - 2))
            for g in range(GQ):
                m = act.do(lambda e, g=g: e.activation(
                    prob[t % 2][:, g, :], bank(2 + t % 2)[:, g * P:(g + 1) * P], ACT.Exp,
                    bias=st_t[:, 1, g:g + 1], scale=SCORE1, accum_out=st_t[:, 2, g:g + 1]), S["exp"])
            M["exp", t] = m

        def normalise(t):
            if not 0 <= t < total:
                return
            st_t = soft[t % 2]
            dve.wait(mark("exp", t))
            m = dve.do(lambda e: e.reciprocal(st_t[:, 3, :], st_t[:, 2, :]), S["rec"])
            dve.wait(m)
            M["norm", t] = dve.do(lambda e: e.tensor_tensor(
                prob[t % 2][:], prob[t % 2][:], st_t[:, 3, :, None].to_broadcast([P, GQ, P]), ALU.mult), S["norm"])

        def turn_prob(t):
            if not 0 <= t < total:
                return
            pe.wait(mark("norm", t), mark("pT_hi", t - 2), mark("pT_lo", t - 2))
            for g in range(GQ):
                m = pe.do(lambda e, g=g: e.transpose(
                    bank(4 + t % 2)[:, g * P:(g + 1) * P], prob[t % 2][:, g, :], ident[:]),
                    S["pT_mm"] if g == GQ - 1 else None)
            M["pT_mm", t] = m

        def split_probT(t):
            if not 0 <= t < total:
                return
            dst = [probT[t // 2 % 2][:, part, t % 2, :, :].rearrange("p g n -> p (g n)") for part in range(2)]
            act.wait(mark("pT_mm", t), mark("pv_mm", t // 2 - 2))
            M["pT_hi", t] = act.do(lambda e: e.copy(dst[0], bank(4 + t % 2)), S["pT_hi"])
            dve.wait(mark("pT_hi", t))
            M["pT_lo", t] = dve.do(lambda e: e.tensor_tensor(dst[1], bank(4 + t % 2), f32(dst[0]), ALU.subtract),
                                   S["pT_lo"])

        def context(pair):
            if not 0 <= pair < total // 2:
                return
            b, r = divmod(pair, UNITS // 2)
            q, side = divmod(r, 2)
            pe.wait(mark("pT_lo", 2 * pair + 1), mark("vp", (b, q)))
            if side == 0:
                pe.wait(mark("c_lo", divmod(b * NQ + q - 1, NQ)))
            ps = bank(6)[:, side * 2 * P:(side + 1) * 2 * P]
            for n, (part, vpart) in enumerate(((0, 0), (0, 1), (1, 0))):
                for g in range(GQ):
                    first, last = n == 0 and g == 0, n == 2 and g == GQ - 1
                    m = pe.do(lambda e, part=part, vpart=vpart, g=g, first=first, last=last: e.matmul(
                        ps, v_pad[:, vpart, q, g, :], probT[pair % 2][:, part, :, g, :],
                        start=first, stop=last), S["pv_mm"] if last else None)
            M["pv_mm", pair] = m

        def split_context(pair):
            if not 0 <= pair < total // 2 or pair % 2 == 0:
                return
            b, r = divmod(pair, UNITS // 2)
            q = r // 2
            dst = [cT[:, part, q * GROUP:(q + 1) * GROUP, :].rearrange("p j n -> p (j n)") for part in range(2)]
            act.wait(mark("pv_mm", pair), mark("o_mm", (b - 1, (q + 1) * GROUP - 1)))
            M["c_hi", (b, q)] = act.do(lambda e: e.copy(dst[0], bank(6)), S["c_hi"])
            dve.wait(mark("c_hi", (b, q)))
            M["c_lo", (b, q)] = dve.do(lambda e: e.tensor_tensor(dst[1], bank(6), f32(dst[0]), ALU.subtract),
                                       S["c_lo"])

        load_h_early(0)

        for t in range(-12, total + UNITS):
            b, s = divmod(t, UNITS)
            scores(t)
            turn_prob(t - 2)
            if (t - 4) % 2 == 0:
                context((t - 4) // 2)
            split_probT(t - 2)
            normalise(t - 1)
            maxima(t)
            exponents(t)
            if (t - 4) % 2 == 0:
                split_context((t - 4) // 2)
            if s == 0:
                turn_q(b, 1)
                split_qT(b, 1)
                keys_diagonal(b, 1)
                load_k(b + 1)
                if b >= 1:
                    load_h_res(b)
            if s == 3:
                values_padded(b, 1)
                load_v(b + 1)
            if s < 4:
                project_q(b + 1, s)
                if s == 3:
                    evacuate_q(b + 1)
            else:
                if s in (4, 5):
                    turn_h(b + 2, s - 4)
                    split_hT(b + 2, s - 4)
                    if s == 5:
                        load_h_early(b + 3)
                if s == 6:
                    turn_q(b + 1, 0)
                    split_qT(b + 1, 0)
                project_o(b - 1, s - 4)
                if s == 4:
                    keys_diagonal(b + 1, 0)
                if s == 7:
                    values_padded(b + 1, 0)
                    finish_out(b - 1)
            if t == -10:
                load_h_res(0)
                for r in range(2):
                    for part, w in ((0, wo_hi), (1, wo_lo)):
                        for c in range(4 * r, 4 * r + 4):
                            M["wo_in", r] = load(f32(w[:, c, :]), wo_dram[part][c], s_wo_in)
        sp.wait(M["out", B - 2], M["out", B - 1])

        with nc.Block() as block:
            @block.tensor
            def _(eng):
                pe.play(eng)

            @block.scalar
            def _(eng):
                act.play(eng)

            @block.vector
            def _(eng):
                dve.play(eng)

            @block.gpsimd
            def _(eng):
                pool.play(eng)

            @block.sync
            def _(eng):
                sp.play(eng)


_INS = ["x", "ctx_4096",
        "L0_xattn_Wq", "L0_xattn_bq", "L0_xattn_Wk", "L0_xattn_bk", "L0_xattn_Wv", "L0_xattn_bv",
        "L0_xattn_Wo", "L0_xattn_bo", "L0_xattn_gn_w", "L0_xattn_gn_b",
        "L1_xattn_Wq", "L1_xattn_Aq", "L1_xattn_Bq", "L1_xattn_Wk", "L1_xattn_Ak", "L1_xattn_Bk",
        "L1_xattn_Wv", "L1_xattn_Av", "L1_xattn_Bv", "L1_xattn_Wo", "L1_xattn_Ao", "L1_xattn_Bo"]


def kernel(**inputs):
    import numpy as np
    import concourse.bacc as bacc
    from concourse.bass_utils import run_bass_kernel_spmd

    nc = bacc.Bacc("TRN2", target_bir_lowering=False, num_devices=1)
    arrays, args = {}, []
    for name in _INS:
        a = np.ascontiguousarray(inputs[name])
        arrays[f"in_{name}"] = a
        args.append(nc.dram_tensor(f"in_{name}", a.shape, mybir.dt.from_np(a.dtype), kind="ExternalInput").ap())
    shape = arrays["in_x"].shape
    out = nc.dram_tensor("out_dram", shape, F32, kind="ExternalOutput").ap()
    xattn_two_layers(nc, *args, out)
    result = run_bass_kernel_spmd(nc, [arrays], core_ids=[0])
    return result.results[0]["out_dram"]
```

```python
from contextlib import ExitStack

import concourse.bass as bass
from concourse import mybir

F32 = mybir.dt.float32
F32R = mybir.dt.float32r
ALU = mybir.AluOpType
ACT = mybir.ActivationFunctionType
AX_X = mybir.AxisListType.X

P = 128
BANK = 512
DMA = 16


class Signal:

    def __init__(self, sem):
        self.sem, self.count = sem, 0

    def mark(self, step):
        self.count += step
        return self, self.count


class Lane:

    def __init__(self):
        self.steps, self.passed = [], {}

    def wait(self, *marks):
        for signal, count in (m for m in marks if m is not None):
            if self.passed.get(signal, 0) < count:
                self.passed[signal] = count
                self.steps.append(lambda eng, s=signal.sem, c=count: eng.wait_ge(s, c))

    def do(self, make, signal=None, step=1):
        if signal is None:
            self.steps.append(make)
            return None
        self.steps.append(lambda eng, s=signal.sem: make(eng).then_inc(s, step))
        return signal.mark(step)

    def play(self, eng):
        for step in self.steps:
            step(eng)


def xattn_two_layers(nc, x, ctx_4096, Wq0, bq0, Wk0, bk0, Wv0, bv0, Wo0, bo0, gn_w, gn_b,
                     Wq, Aq, Bq, Wk, Ak, Bk, Wv, Av, Bv, Wo, Ao, Bo, out):
    B, E, L = x.shape
    HID = Wq.shape[1]
    KV = Wk.shape[1]
    R = Aq.shape[1]
    NC = HID // P
    HALF = HID // 2
    H0, D0 = 8, E // 8
    NH, HD = 32, HID // 32
    NKV = KV // HD
    GROUP = NH // NKV
    GQ = P // HD
    NQ = NKV // GQ
    UNITS = NQ * GROUP
    LORA_SCALE = 32.0 / 16.0
    SCORE0 = float(E) ** -0.5
    SCORE1 = float(HD) ** -0.5
    EPS = 1e-5
    OFF_BLOCK = -1e30
    assert E == P and HALF == BANK and 2 * KV == BANK and GQ * P == BANK and L == HID

    with ExitStack() as ctx:
        end = nc.sbuf_usable_end
        start = (nc.sbuf_base + 63) // 64 * 64
        at = [start]

        def sb(name, shape, dt=F32):
            size = 4
            for n in shape[1:]:
                size *= n
            a = at[0]
            at[0] = a + (size + 31) // 32 * 32
            assert at[0] <= end, (name, at[0], end)
            return nc.alloc_sbuf_tensor_at(name, shape, dt, offset=a)

        def signal(name):
            return Signal(ctx.enter_context(nc.semaphore(name)))

        def scratch(name, shape, dt=F32):
            return nc.dram_tensor(name, shape, dt, kind="Internal").ap()

        pe, act, dve, pool, sp = Lane(), Lane(), Lane(), Lane(), Lane()

        h_dram = scratch("h_dram", (B, P, HID))
        kT_dram = scratch("kT_dram", (B, P, KV // P * P))
        v_dram = scratch("v_dram", (B, P, KV))
        wo_dram = [scratch(f"wo_{s}_dram", (NC, P, HID)) for s in ("hi", "lo")]

        ident = sb("ident", [P, P])
        w_place = at[0]
        wq_hi = sb("wq_hi", [P, NC, HID], F32R)
        wq_lo = sb("wq_lo", [P, NC, HID], F32R)
        shared = at[0]

        wkv_hi = sb("wkv_hi", [P, NC, 2 * KV], F32R)
        wkv_lo = sb("wkv_lo", [P, NC, 2 * KV], F32R)
        y_in = [sb(f"y_in{i}", [P, L]) for i in range(2)]
        yT = [sb(f"yT{i}", [P, NC, 2 * P + 2], F32R) for i in range(2)]
        x_in = [sb(f"x_in{i}", [P, L]) for i in range(2)]
        x_hi = sb("x_hi", [P, L], F32R)
        x_lo = sb("x_lo", [P, L], F32R)
        h_out = [sb(f"h_out{i}", [P, L]) for i in range(2)]
        kv_sb = [sb(f"kv_sb{i}", [P, 2 * KV]) for i in range(2)]
        kT_sb = [sb(f"kT_sb{i}", [P, KV]) for i in range(2)]
        w_raw = [sb(f"w_raw{i}", [P, BANK]) for i in range(2)]
        o_split = [sb(f"o_split{i}", [P, 2, BANK], F32R) for i in range(2)]
        lora_cols = {"kv": 2 * KV, "q": HID, "o": HID}
        lora_aT = {m: sb(f"lora_aT_{m}", [P, HID], F32R) for m in lora_cols}
        lora_b = {m: sb(f"lora_b_{m}", [P, n], F32R) for m, n in lora_cols.items()}
        ones_avg = sb("ones_avg", [P, P])
        w0T = sb("w0T", [P, 3, P])
        wv0 = sb("wv0", [P, P])
        bias_rows = sb("bias_rows", [1, 2, P])
        ones_row = sb("ones_row", [1, P])
        bqk = sb("bqk", [P, 2, P])
        score_bias = sb("score_bias", [P, P])
        columns = sb("columns", [P, 5])
        bq_col, bv_col, bo_col, gnw_col, gnb_col = (columns[:, i:i + 1] for i in range(5))
        bq_scaled = sb("bq_scaled", [P, 1])
        minus_half = sb("minus_half", [P, 1])
        gram_right = [sb(f"gram_right{i}", [P, P + 1]) for i in range(2)]
        gram = sb("gram", [P, P])
        t1 = sb("t1", [P, P])
        s_bq = sb("s_bq", [P, P])
        att = sb("att", [P, P])
        n1 = sb("n1", [P, P])
        mix = sb("mix", [P, P])
        mix_split = sb("mix_split", [P, 2, P], F32R)
        att_stat = sb("att_stat", [P, 4])
        norm = sb("norm", [P, 16])
        bn = sb("bn", [P, 2, 6])

        at[0] = w_place
        wkv_raw = sb("wkv_raw", [P, NC, 2 * KV])
        w0_raw = sb("w0_raw", [P, 3, P])
        lora_a = {m: sb(f"lora_a_{m}", [P, NC, 2 * R]) for m in lora_cols}
        lora_a3 = {m: sb(f"lora_a3_{m}", [P, NC, P]) for m in lora_cols}
        lora_b3 = {m: sb(f"lora_b3_{m}", [P, n]) for m, n in lora_cols.items()}
        assert at[0] <= shared

        at[0] = shared
        hT = sb("hT", [P, 2, NC, P], F32R)
        h_in = sb("h_in", [P, HID])
        q_sb = sb("q_sb", [P, HID])
        qT = sb("qT", [P, 2, UNITS, P], F32R)
        k_diag = sb("k_diag", [P, 2, NQ, GQ, P], F32R)
        k_in = sb("k_in", [P, NQ, P])
        v_in = sb("v_in", [P, NQ, GQ, HD])
        wo_hi = sb("wo_hi", [P, NC, HID], F32R)
        wo_lo = sb("wo_lo", [P, NC, HID], F32R)
        prob = [sb(f"prob{i}", [P, GQ, P]) for i in range(2)]
        probT = [sb(f"probT{i}", [P, GROUP, GQ, P]) for i in range(2)]
        cT = sb("cT", [P, 2, UNITS, P], F32R)
        soft = [sb(f"soft{i}", [P, 4, GQ]) for i in range(2)]

        banks = [ctx.enter_context(nc.psum_tensor(f"bank{i}", [P, 2 * BANK], F32)) for i in range(4)]

        def bank(i):
            return banks[i // 2][:, i % 2 * BANK:(i % 2 + 1) * BANK]

        def f32(ap):
            return ap.bitcast(F32)

        s_const = signal("s_const")
        s_pool = signal("s_pool")
        s_pe0 = signal("s_pe0")
        s_act0 = signal("s_act0")
        s_dve0 = signal("s_dve0")

        ident_zero = pool.do(lambda e: e.memset(ident[:], 0.0), s_pool)
        mask_zero = pool.do(lambda e: e.memset(score_bias[:], 0.0), s_pool)
        pool.wait(ident_zero)
        ident_ok = pool.do(lambda e: e.affine_select(
            out=ident[:], in_=ident[:], compare_op=ALU.not_equal, fill=1.0, base=0,
            pattern=[[-1, P]], channel_multiplier=1), s_pool)
        mask = score_bias[:].rearrange("p (b e) -> p b e", b=H0)
        pool.wait(mask_zero)
        above = pool.do(lambda e: e.affine_select(
            out=mask, in_=mask, compare_op=ALU.is_ge, fill=OFF_BLOCK, base=0,
            pattern=[[-D0, H0], [0, D0]], channel_multiplier=1), s_pool)
        pool.wait(above)
        mask_ok = pool.do(lambda e: e.affine_select(
            out=mask, in_=mask, compare_op=ALU.is_ge, fill=OFF_BLOCK, base=D0 - 1,
            pattern=[[D0, H0], [0, D0]], channel_multiplier=-1), s_pool)
        ones_ok = pool.do(lambda e: e.memset(ones_row[:], 1.0), s_pool)
        pool.do(lambda e: e.memset(minus_half[:], -0.5), s_pool)
        avg_ok = pool.do(lambda e: e.memset(ones_avg[:], 1.0 / P), s_pool)
        for i in range(2):
            yT_ones = pool.do(lambda e, i=i: e.memset(yT[i][:, :, 2 * P:2 * P + 2].bitcast(F32), 1.0), s_pool)

        def load(dst, src, sig):
            return sp.do(lambda e: e.dma_start(dst, src), sig, DMA)

        s_y = [signal(f"s_y{i}") for i in range(2)]
        s_x = [signal(f"s_x{i}") for i in range(2)]
        s_wraw = [signal(f"s_wraw{i}") for i in range(2)]
        s_lora = signal("s_lora")
        s_w0 = signal("s_w0")

        factors = {"kv": ((Ak, 0, Bk, 0), (Av, R, Bv, KV)), "q": ((Aq, 0, Bq, 0),), "o": ((Ao, 0, Bo, 0),)}
        lora_zero, lora_loaded = {}, {}
        for m in factors:
            pool.do(lambda e, m=m: e.memset(lora_b3[m][:], 0.0))
            lora_zero[m] = pool.do(lambda e, m=m: e.memset(lora_a3[m][:], 0.0), s_pool)

        def load_lora(m):
            sig = signal(f"s_lora_{m}")
            for a, first, b, col in factors[m]:
                if m == "o":
                    rows = a.rearrange("(q g j d) r -> q g d j r", q=NQ, g=GQ, j=GROUP)
                    for q in range(NQ):
                        for g in range(GQ):
                            load(lora_a[m][g * HD:(g + 1) * HD, q * GROUP:(q + 1) * GROUP, first:first + R],
                                 rows[q, g], sig)
                else:
                    load(lora_a[m][:, :, first:first + R], a.rearrange("(c p) r -> p c r", p=P), sig)
            sp.wait(lora_zero[m])
            for a, first, b, col in factors[m]:
                for q in range(3):
                    lora_loaded[m] = load(
                        lora_b3[m][32 * q + first:32 * q + first + R, col:col + b.shape[1]], b, sig)

        s_wkv = signal("s_wkv")
        y_loaded = {0: load(y_in[0][:], ctx_4096[0], s_y[0])}
        load_lora("kv")
        load(wkv_raw[:, :, 0:KV], Wk.rearrange("(c p) n -> p c n", p=P), s_wkv)
        wkv_loaded = load(wkv_raw[:, :, KV:2 * KV], Wv.rearrange("(c p) n -> p c n", p=P), s_wkv)
        for dst, src in ((w0_raw[:, 0, :], Wq0), (w0_raw[:, 1, :], Wk0), (w0_raw[:, 2, :], Wo0), (wv0[:], Wv0)):
            load(dst, src, s_w0)
        for row, src in ((0, bq0), (1, bk0)):
            load(bias_rows[:, row, :], src.rearrange("(a n) -> a n", a=1), s_w0)
        for col, src in ((bq_col, bq0), (bv_col, bv0), (bo_col, bo0), (gnw_col, gn_w), (gnb_col, gn_b)):
            w0_loaded = load(col, src.rearrange("(n a) -> n a", a=1), s_w0)

        lora_ready = {}
        turned_free = {0: None, 1: None}

        def stack_lora(m):
            n = lora_cols[m]
            used = R * len(factors[m])
            dve.wait(lora_loaded[m], lora_zero[m])
            for q in range(3):
                a3_ok = dve.do(lambda e, q=q: e.tensor_copy(
                    lora_a3[m][:, :, 32 * q:32 * q + used], lora_a[m][:, :, 0:used]), s_dve0)
            hi = dve.do(lambda e: e.tensor_copy(lora_b[m][:], lora_b3[m][:]), s_dve0)
            dve.wait(hi)
            dve.do(lambda e: e.tensor_tensor(
                lora_b[m][64:96, :], lora_b3[m][64:96, :], f32(lora_b[m][64:96, :]), ALU.subtract), s_dve0)
            pe.wait(a3_ok, ident_ok)
            for half in range(2):
                pe.wait(turned_free[half])
                for c in range(4):
                    turned = pe.do(lambda e, half=half, c=c: e.transpose(
                        bank(4 + half)[:, c * P:(c + 1) * P], lora_a3[m][:, 4 * half + c, :], ident[:]), s_pe0)
                dst = lora_aT[m][:, half * BANK:(half + 1) * BANK]
                dve.wait(turned)
                hi = dve.do(lambda e, dst=dst, half=half: e.tensor_copy(dst, bank(4 + half)), s_dve0)
                dve.wait(hi)
                turned_free[half] = lora_ready[m] = dve.do(lambda e, dst=dst, half=half: e.tensor_tensor(
                    dst[32:64, :], bank(4 + half)[32:64, :], f32(dst[32:64, :]), ALU.subtract), s_dve0)

        stack_lora("kv")

        def prepare_layer0():
            pe.wait(w0_loaded, ident_ok, ones_ok)
            for i in range(3):
                turned = pe.do(lambda e, i=i: e.transpose(
                    bank(3)[:, i * P:(i + 1) * P], w0_raw[:, i, :], ident[:]), s_pe0)
            act.wait(turned)
            w0T_ok = act.do(lambda e: e.copy(w0T[:].rearrange("p a b -> p (a b)"), bank(3)[:, 0:3 * P]), s_act0)
            pe.wait(w0T_ok)
            for i in range(2):
                spread = pe.do(lambda e, i=i: e.matmul(bank(3)[:, i * P:(i + 1) * P], ones_row[:],
                                                       bias_rows[:, i, :], start=True, stop=True), s_pe0)
            act.wait(spread)
            bqk_ok = act.do(lambda e: e.copy(bqk[:].rearrange("p a b -> p (a b)"), bank(3)[:, 0:2 * P]), s_act0)
            dve.wait(bqk_ok, mask_ok, w0_loaded)
            scaled = dve.do(lambda e: e.tensor_scalar(bq_scaled[:], bq_col, SCORE0 * L, None, ALU.mult), s_dve0)
            dve.wait(scaled)
            bias_ok = dve.do(lambda e: e.scalar_tensor_tensor(
                score_bias[:], bqk[:, 1, :], bq_scaled[:], score_bias[:], ALU.mult, ALU.add), s_dve0)
            return w0T_ok, bqk_ok, bias_ok

        wqT0, wkT0, woT0 = (w0T[:, i, :] for i in range(3))

        small_free = [None, None]
        small_turn = [0]

        def small_bank():
            i = small_turn[0] % 2
            small_turn[0] += 1
            pe.wait(small_free[i])
            return i, bank(6 + i)

        M = {}

        def mark(stage, b):
            return M.get((stage, b))

        s_prep = signal("s_prep")
        s_prep_w = signal("s_prep_w")
        s_prep_hi = signal("s_prep_hi")
        s_prep_lo = signal("s_prep_lo")
        s_prep_lo_dve = signal("s_prep_lo_dve")
        s_wo_out = [signal(f"s_wo_out{i}") for i in range(2)]
        raw_free = [None, None]
        raw_loaded = {}
        o_stored = [None, None]
        units = [("kv", c, 0) for c in range(NC)]
        units += [(m, c, half) for m in ("q", "o") for c in range(NC) for half in range(2)]

        def raw_piece(n):
            return wkv_raw[:, units[n][1], :] if units[n][0] == "kv" else w_raw[n % 2][:]

        def load_raw(n):
            if n >= len(units):
                return
            m, c, half = units[n]
            i = n % 2
            sp.wait(raw_free[i])
            columns_of = slice(half * BANK, (half + 1) * BANK)
            if m == "q":
                raw_loaded[n] = load(w_raw[i][:], Wq[c * P:(c + 1) * P, columns_of], s_wraw[i])
            else:
                rows = Wo.rearrange("(q g j d) n -> q j g d n", q=NQ, g=GQ, j=GROUP)[c // GROUP, c % GROUP]
                for g in range(GQ):
                    raw_loaded[n] = load(w_raw[i][g * HD:(g + 1) * HD, :], rows[g, :, columns_of], s_wraw[i])

        prep_at = {}

        def prep_product(n):
            m, c, half = units[n]
            i, ps = small_bank()
            pe.wait(lora_ready[m])
            prep_at[n] = i, pe.do(lambda e: e.matmul(
                ps, lora_aT[m][:, c * P:(c + 1) * P], lora_b[m][:, half * BANK:(half + 1) * BANK],
                start=True, stop=True), s_prep)

        def prep_merge(n):
            i, product = prep_at[n]
            raw = raw_piece(n)
            dve.wait(product, wkv_loaded if units[n][0] == "kv" else raw_loaded[n])
            small_free[i] = dve.do(lambda e: e.scalar_tensor_tensor(
                raw, bank(6 + i), LORA_SCALE, raw, ALU.mult, ALU.add), s_prep_w)
            return small_free[i]

        def prep_parts(n):
            m, c, half = units[n]
            raw = raw_piece(n)
            if m == "kv":
                return raw, wkv_hi[:, c, :], wkv_lo[:, c, :]
            if m == "q":
                hi, lo = (w[:, c, half * BANK:(half + 1) * BANK].rearrange(
                    "p (j g d) -> p g j d", g=GQ, j=GROUP) for w in (wq_hi, wq_lo))
                return raw.rearrange("p (g j d) -> p g j d", g=GQ, j=GROUP), hi, lo
            return raw, o_split[n % 2][:, 0, :], o_split[n % 2][:, 1, :]

        def prep_round(n, merged):
            m = units[n][0]
            raw, hi, lo = prep_parts(n)
            act.wait(merged)
            if m == "q":
                act.wait(lora_ready["o"], w0T_ok, *wkv_ok)
            if m == "o":
                act.wait(o_stored[n % 2])
            return act.do(lambda e: e.copy(hi, raw), s_prep_hi)

        def prep_rest(n, rounded, lane, sig):
            m, c, half = units[n]
            raw, hi, lo = prep_parts(n)
            lane.wait(rounded)
            lo_ok = lane.do(lambda e: e.tensor_tensor(lo, raw, f32(hi), ALU.subtract), sig)
            if m != "kv":
                raw_free[n % 2] = lo_ok
            if m == "o":
                sp.wait(lo_ok)
                for part in range(2):
                    o_stored[n % 2] = sp.do(lambda e, part=part: e.dma_start(
                        wo_dram[part][c, :, half * BANK:(half + 1) * BANK], f32(o_split[n % 2][:, part, :])),
                        s_wo_out[n % 2], DMA)
            return lo_ok

        wkv_ok = []
        next_unit = [NC]

        names_a = ("yT_mm", "yT_hi", "yT_lo", "gram_mm", "gram_r", "gram", "t1_mm", "t1", "sbq",
                   "s_mm", "s_sb", "s_max", "s_neg", "s_exp", "s_rec", "att", "n1_mm", "n1", "mix_mm",
                   "mix", "mix_hi", "mix_lo", "xbias", "x_hi", "x_lo", "mx_mm", "bn", "agg", "st",
                   "st1_mm", "dev", "nm", "st2", "st2_mm", "ve", "pow", "gsc", "gbi", "h", "kv_mm",
                   "kv", "kT_mm", "kT")
        S = {n: signal("a_" + n) for n in names_a}
        s_h_out = [signal(f"s_h_out{i}") for i in range(2)]
        s_kv_out = [signal(f"s_kv_out{i}") for i in range(2)]

        def load_y(b):
            if 0 < b < B:
                sp.wait(mark("yT_mm", (b - 2, 1)))
                y_loaded[b] = load(y_in[b % 2][:], ctx_4096[b], s_y[b % 2])

        x_loaded = {}

        def load_x(b):
            if b < B:
                sp.wait(mark("x_hi", b - 2), mark("x_lo", b - 2))
                x_loaded[b] = load(x_in[b % 2][:], x[b], s_x[b % 2])

        def turn_y(b):
            if b >= B:
                return
            pe.wait(y_loaded[b], ident_ok, mark("yT_lo", (b - 1, 1)))
            for c in range(NC):
                m = pe.do(lambda e, c=c: e.transpose(
                    banks[0][:, c * P:(c + 1) * P], y_in[b % 2][:, c * P:(c + 1) * P], ident[:]),
                    S["yT_mm"] if c % 4 == 3 else None)
                M["yT_mm", (b, c // 4)] = m

        def yT_part(b, half, part):
            return (bank(half).rearrange("p (c n) -> p c n", c=4),
                    yT[b % 2][:, 4 * half:4 * half + 4, part * P:(part + 1) * P])

        def round_yT(b, half):
            if b >= B:
                return
            src, hi = yT_part(b, half, 0)
            act.wait(mark("yT_mm", (b, half)), mark("kv_mm", b - 2), mark("gram_mm", b - 2))
            M["yT_hi", (b, half)] = act.do(lambda e: e.copy(hi, src), S["yT_hi"])

        def rest_yT(b, half):
            if b >= B:
                return
            src, hi = yT_part(b, half, 0)
            lo = yT_part(b, half, 1)[1]
            dve.wait(mark("yT_hi", (b, half)))
            M["yT_lo", (b, half)] = dve.do(lambda e: e.tensor_tensor(lo, src, f32(hi), ALU.subtract), S["yT_lo"])

        def kv_products(b, chunks):
            pe.wait(mark("kv", b - 1))
            for c in chunks:
                pe.wait(mark("yT_lo", (b, c // 4)), wkv_ok[c])
                for part, w in ((0, wkv_hi), (0, wkv_lo), (1, wkv_hi)):
                    first = c == 0 and part == 0 and w is wkv_hi
                    last = c == NC - 1 and part == 1
                    m = pe.do(lambda e, c=c, part=part, w=w, first=first, last=last: e.matmul(
                        bank(2), yT[b % 2][:, c, part * P:(part + 1) * P], w[:, c, :], start=first, stop=last),
                        S["kv_mm"] if last else None)
            M["kv_mm", b] = m

        def gram_products(b):
            pe.wait(yT_ones, mark("gram_r", b - 1), mark("gram", b - 1), w0T_ok, bqk_ok)
            for c in range(NC):
                pe.wait(mark("yT_lo", (b, c // 4)))
                for part in range(2):
                    last = c == NC - 1 and part == 1
                    m = pe.do(lambda e, c=c, part=part, last=last: e.matmul(
                        bank(3)[:, 0:2 * P + 2], yT[b % 2][:, c, part * P:(part + 1) * P], yT[b % 2][:, c, :],
                        start=c == 0 and part == 0, stop=last), S["gram_mm"] if last else None)
            M["gram_mm", b] = m

        def sum_gram(b):
            right = gram_right[b % 2]
            act.wait(mark("gram_mm", b), mark("gram", b - 2), mark("sbq", b - 2))
            M["gram_r", b] = act.do(lambda e: e.copy(right[:], bank(3)[:, P:2 * P + 1]), S["gram_r"])
            dve.wait(mark("gram_r", b), mark("t1_mm", b - 1))
            M["gram", b] = dve.do(lambda e: e.tensor_tensor(
                gram[:], bank(3)[:, 0:P], right[:, 0:P], ALU.add), S["gram"])

        def small_product(stage, b, lhsT, rhs, *waits):
            i, ps = small_bank()
            pe.wait(*waits)
            M[stage, b] = pe.do(lambda e: e.matmul(ps[:, 0:rhs.shape[1]], lhsT, rhs, start=True, stop=True),
                                S[stage])
            return i

        held = {}

        def t1_product(b):
            held["t1", b] = small_product("t1_mm", b, gram[:], wkT0, mark("gram", b))

        def evacuate_t1(b):
            i = held["t1", b]
            s = gram_right[b % 2][:, P:P + 1]
            dve.wait(mark("t1_mm", b), mark("s_mm", b - 1), bqk_ok)
            small_free[i] = M["t1", b] = dve.do(lambda e: e.scalar_tensor_tensor(
                t1[:], bqk[:, 1, :], s, bank(6 + i)[:, 0:P], ALU.mult, ALU.add), S["t1"])
            M["sbq", b] = dve.do(lambda e: e.tensor_scalar(s_bq[:], bqk[:, 0, :], s, None, ALU.mult), S["sbq"])

        def score_product(b):
            i, ps = small_bank()
            pe.wait(mark("t1", b), mark("sbq", b))
            pe.do(lambda e: e.matmul(ps[:, 0:P], wqT0, t1[:], start=True, stop=False))
            M["s_mm", b] = pe.do(lambda e: e.matmul(ps[:, 0:P], s_bq[:], wkT0, start=False, stop=True), S["s_mm"])
            held["s", b] = i

        def softmax0_begin(b):
            i = held["s", b]
            dve.wait(mark("s_mm", b), score_bias_ok, mark("n1_mm", b - 1))
            small_free[i] = dve.do(lambda e: e.scalar_tensor_tensor(
                att[:], bank(6 + i)[:, 0:P], SCORE0, score_bias[:], ALU.mult, ALU.add), S["s_sb"])
            dve.wait(small_free[i])
            top = dve.do(lambda e: e.tensor_reduce(att_stat[:, 0:1], att[:], AX_X, ALU.max), S["s_max"])
            dve.wait(top)
            neg = dve.do(lambda e: e.tensor_scalar(att_stat[:, 1:2], att_stat[:, 0:1], -1.0, None, ALU.mult),
                         S["s_neg"])
            act.wait(neg)
            M["s_exp", b] = act.do(lambda e: e.activation(
                att[:], att[:], ACT.Exp, bias=att_stat[:, 1:2], scale=1.0, accum_out=att_stat[:, 2:3]),
                S["s_exp"])

        def softmax0_end(b):
            dve.wait(mark("s_exp", b))
            inverse = dve.do(lambda e: e.reciprocal(att_stat[:, 3:4], att_stat[:, 2:3]), S["s_rec"])
            dve.wait(inverse)
            M["att", b] = dve.do(lambda e: e.tensor_scalar(att[:], att[:], att_stat[:, 3:4], None, ALU.mult),
                                 S["att"])

        def n1_product(b):
            held["n1", b] = small_product("n1_mm", b, att[:], woT0, mark("att", b))

        def evacuate_n1(b):
            i = held["n1", b]
            act.wait(mark("n1_mm", b), mark("mix_mm", b - 1))
            small_free[i] = M["n1", b] = act.do(lambda e: e.copy(n1[:], bank(6 + i)[:, 0:P]), S["n1"])

        def mix_product(b):
            i, ps = small_bank()
            pe.wait(mark("n1", b))
            pe.do(lambda e: e.matmul(ps[:, 0:P], wv0[:], n1[:], start=True, stop=True))
            M["mix_mm", b] = pe.do(lambda e: e.matmul(ps[:, P:P + 1], n1[:], bv_col, start=True, stop=True),
                                   S["mix_mm"])
            held["mix", b] = i

        xbias, mv, st, dev, nm, st2, ve, rstd, gsc, gbi = (
            norm[:, 0:1], norm[:, 1:3], norm[:, 3:4], norm[:, 4:5], norm[:, 5:6], norm[:, 6:7],
            norm[:, 7:8], norm[:, 8:9], norm[:, 9:10], norm[:, 10:11])

        def split_mix(b):
            i = held["mix", b]
            dve.wait(mark("mix_mm", b), mark("mx_mm", b - 1))
            M["mix", b] = dve.do(lambda e: e.tensor_tensor(mix[:], bank(6 + i)[:, 0:P], ident[:], ALU.add), S["mix"])
            small_free[i] = M["xbias", b] = dve.do(lambda e: e.tensor_tensor(
                xbias, bank(6 + i)[:, P:P + 1], bo_col, ALU.add), S["xbias"])
            dve.wait(mark("mix", b))
            M["mix_hi", b] = dve.do(lambda e: e.tensor_copy(mix_split[:, 0, :], mix[:]), S["mix_hi"])
            dve.wait(mark("mix_hi", b))
            M["mix_lo", b] = dve.do(lambda e: e.tensor_tensor(
                mix_split[:, 1, :], mix[:], f32(mix_split[:, 0, :]), ALU.subtract), S["mix_lo"])

        def split_x(b):
            if not 0 <= b < B:
                return
            act.wait(x_loaded[b], mark("mx_mm", b - 1))
            M["x_hi", b] = act.do(lambda e: e.copy(x_hi[:], x_in[b % 2][:]), S["x_hi"])
            pool.wait(mark("x_hi", b))
            M["x_lo", b] = pool.do(lambda e: e.tensor_tensor(x_lo[:], x_in[b % 2][:], f32(x_hi[:]), ALU.subtract),
                                  S["x_lo"])

        def mixed_x(b):
            pe.wait(mark("mix_lo", b), mark("x_lo", b), mark("h", b - 1), *turned_free.values())
            for part, xs in ((0, x_hi), (0, x_lo), (1, x_hi)):
                for half in range(2):
                    first, last = part == 0 and xs is x_hi, part == 1
                    m = pe.do(lambda e, part=part, xs=xs, half=half, first=first, last=last: e.matmul(
                        bank(4 + half), mix_split[:, part, :], xs[:, half * BANK:(half + 1) * BANK],
                        start=first, stop=last), S["mx_mm"] if last and half else None)
            M["mx_mm", b] = m

        def partition_stats(b):
            dve.wait(mark("mx_mm", b), mark("xbias", b))
            for half in range(2):
                m = dve.do(lambda e, half=half: e.bn_stats(bn[:, half, :], bank(4 + half)), S["bn"])
            dve.wait(m)
            m = dve.do(lambda e: e.bn_aggr(mv, bn[:].rearrange("p a b -> p (a b)")), S["agg"])
            dve.wait(m)
            M["st", b] = dve.do(lambda e: e.tensor_tensor(st, mv[:, 0:1], xbias, ALU.add), S["st"])

        def mean_product(b):
            held["st1", b] = small_product("st1_mm", b, ones_avg[:], st, mark("st", b), avg_ok)

        def deviation(b):
            i = held["st1", b]
            mean = bank(6 + i)[:, 0:1]
            dve.wait(mark("st1_mm", b))
            m = dve.do(lambda e: e.tensor_tensor(dev, st, mean, ALU.subtract), S["dev"])
            small_free[i] = M["nm", b] = dve.do(lambda e: e.tensor_tensor(nm, xbias, mean, ALU.subtract), S["nm"])
            dve.wait(m)
            M["st2", b] = dve.do(lambda e: e.scalar_tensor_tensor(st2, dev, dev, mv[:, 1:2], ALU.mult, ALU.add),
                                 S["st2"])

        def var_product(b):
            held["st2", b] = small_product("st2_mm", b, ones_avg[:], st2, mark("st2", b))

        def norm_factors(b):
            i = held["st2", b]
            dve.wait(mark("st2_mm", b), mark("h", b - 1))
            small_free[i] = m = dve.do(lambda e: e.tensor_scalar(ve, bank(6 + i)[:, 0:1], EPS, None, ALU.add), S["ve"])
            pool.wait(m)
            m = pool.do(lambda e: e.tensor_tensor(rstd, ve, minus_half[:], ALU.pow), S["pow"])
            M["pow", b] = m

        def norm_scale(b):
            dve.wait(mark("pow", b), w0_loaded)
            m = dve.do(lambda e: e.tensor_tensor(gsc, rstd, gnw_col, ALU.mult), S["gsc"])
            dve.wait(m, mark("nm", b))
            M["gbi", b] = dve.do(lambda e: e.scalar_tensor_tensor(gbi, nm, gsc, gnb_col, ALU.mult, ALU.add), S["gbi"])

        h_stored = {}
        kv_stored = {}

        def write_h(b):
            act.wait(mark("gbi", b), mark("mx_mm", b), h_stored.get(b - 2))
            M["h", b] = act.do(lambda e: e.activation(
                h_out[b % 2][:], banks[2][:], ACT.Identity, bias=gbi, scale=gsc), S["h"])
            sp.wait(mark("h", b))
            h_stored[b] = sp.do(lambda e: e.dma_start(h_dram[b], h_out[b % 2][:]), s_h_out[b % 2], DMA)

        def evacuate_kv(b):
            act.wait(mark("kv_mm", b), kv_stored.get(b - 2), mark("kT_mm", b - 2))
            M["kv", b] = act.do(lambda e: e.copy(kv_sb[b % 2][:], bank(2)), S["kv"])

        def turn_k(b):
            i, ps = small_bank()
            pe.wait(mark("kv", b))
            for c in range(KV // P):
                m = pe.do(lambda e, c=c: e.transpose(
                    ps[:, c * P:(c + 1) * P], kv_sb[b % 2][:, c * P:(c + 1) * P], ident[:]),
                    S["kT_mm"] if c == KV // P - 1 else None)
            M["kT_mm", b] = m
            held["kT", b] = i

        def evacuate_kT(b):
            i = held["kT", b]
            act.wait(mark("kT_mm", b), kv_stored.get(b - 2))
            small_free[i] = M["kT", b] = act.do(lambda e: e.copy(kT_sb[b % 2][:], bank(6 + i)[:, 0:KV]), S["kT"])
            sp.wait(mark("kv", b), mark("kT", b))
            sp.do(lambda e: e.dma_start(v_dram[b], kv_sb[b % 2][:, KV:2 * KV]), s_kv_out[b % 2], DMA)
            kv_stored[b] = sp.do(lambda e: e.dma_start(kT_dram[b], kT_sb[b % 2][:]), s_kv_out[b % 2], DMA)

        load_y(1)
        load_lora("q")
        load_x(0)
        load_lora("o")
        load_raw(NC)
        load_raw(NC + 1)
        turn_y(0)
        for half in range(2):
            round_yT(0, half)
            rest_yT(0, half)
        w0T_ok, bqk_ok, score_bias_ok = prepare_layer0()
        prep_product(0)
        rounded = prep_round(0, prep_merge(0))
        for n in range(NC):
            if n + 1 < NC:
                prep_product(n + 1)
                merged = prep_merge(n + 1)
            wkv_ok.append(prep_rest(n, rounded, *((dve, s_prep_lo_dve) if n % 2 else (pool, s_prep_lo))))
            if n + 1 < NC:
                rounded = prep_round(n + 1, merged)
        UNIT_EXTRA = 3

        def sequence_a(b):
            old = b > 0
            gram_products(b)
            if old:
                partition_stats(b - 1)
            split_x(b)
            sum_gram(b)
            load_y(b + 2)
            load_x(b + 1)
            kv_products(b, (0,))
            if old:
                mean_product(b - 1)
                deviation(b - 1)
            kv_products(b, (1,))
            t1_product(b)
            evacuate_t1(b)
            kv_products(b, (2,))
            if old:
                var_product(b - 1)
                norm_factors(b - 1)
            else:
                stack_lora("q")
            score_product(b)
            turn_y(b + 1)
            round_yT(b + 1, 0)
            softmax0_begin(b)
            rest_yT(b + 1, 0)
            round_yT(b + 1, 1)
            softmax0_end(b)
            rest_yT(b + 1, 1)
            if old:
                norm_scale(b - 1)
            else:
                stack_lora("o")
            kv_products(b, (3, 4, 5))
            n1_product(b)
            evacuate_n1(b)
            if old:
                write_h(b - 1)
            kv_products(b, (6,))
            mix_product(b)
            split_mix(b)
            kv_products(b, (7,))
            evacuate_kv(b)
            if old:
                turn_k(b - 1)
                evacuate_kT(b - 1)
            units_now = 0 if b == 0 else 2 if b == UNIT_EXTRA else 1
            for n in range(next_unit[0], next_unit[0] + units_now):
                prep_product(n)
                prep_rest(n, prep_round(n, prep_merge(n)), pool, s_prep_lo)
                load_raw(n + 2)
            next_unit[0] += units_now
            mixed_x(b)

        for b in range(B):
            sequence_a(b)
        assert next_unit[0] == len(units)

        early = [mark("kv_mm", B - 1), mark("gram_mm", B - 1), mark("yT_mm", (B - 1, 1)),
                 mark("yT_lo", (B - 1, 1)), mark("gram", B - 1), mark("gram_r", B - 1), mark("kv", B - 1)]

        s_wo_in = signal("s_wo_in")
        s_he = signal("s_he")
        s_hr = signal("s_hr")
        s_k = signal("s_k")
        s_v = [signal(f"s_v{q}") for q in range(NQ)]
        s_out = signal("s_out")
        names_b = ("kd", "hT_mm", "hT_hi", "hT_lo", "q_mm", "q", "qT_mm", "qT_hi", "qT_lo", "sc_mm",
                   "max", "neg", "exp", "rec", "norm", "pT_mm", "pT", "pv_mm", "c_hi", "c_lo",
                   "o_mm", "o")
        S.update({n: signal("b_" + n) for n in names_b})

        pool.wait(*early)
        zeros_ok = pool.do(lambda e: e.memset(k_diag[:].bitcast(F32), 0.0), s_pool)
        pool.wait(zeros_ok)

        def in_range(b):
            return 0 <= b < B

        def load_h_early(b):
            if in_range(b):
                sp.wait(mark("hT_mm", (b - 1, 1)), mark("out", b - 4))
                M["h_early", b] = load(h_in[:], h_dram[b], s_he)

        def load_h_res(b):
            if in_range(b):
                sp.wait(mark("hT_mm", (min(b + 3, B - 1), 1)), mark("out", b - 1))
                M["h_res", b] = load(h_in[:], h_dram[b], s_hr)

        def load_k(b):
            if in_range(b):
                sp.wait(mark("kd", (b - 1, NQ - 1)))
                M["k_in", b] = load(k_in[:], kT_dram[b].rearrange("p (q t) -> p q t", q=NQ), s_k)

        def load_v(b, q):
            if in_range(b):
                sp.wait(mark("pv_mm", (b - 1, q)))
                M["v_in", (b, q)] = load(v_in[:, q, :, :], v_dram[b][:, q * P:(q + 1) * P].rearrange(
                    "p (g d) -> p g d", g=GQ), s_v[q])

        def after_pool(*marks):
            pool.wait(M.get("pool"), *marks)

        def keys_diagonal(b, q):
            if not in_range(b):
                return
            pool.wait(M["k_in", b], mark("sc_mm", (b - 1) * UNITS + (q + 1) * GROUP - 1))
            for g in range(GQ):
                rows = slice(g * HD, (g + 1) * HD)
                after_pool()
                M["pool"] = pool.do(lambda e, rows=rows, g=g: e.tensor_scalar(
                    k_diag[rows, 0, q, g, :], k_in[rows, q, :], 1.0, None, ALU.mult), S["kd"])
                after_pool()
                M["pool"] = pool.do(lambda e, rows=rows, g=g: e.tensor_tensor(
                    k_diag[rows, 1, q, g, :], k_in[rows, q, :], f32(k_diag[rows, 0, q, g, :]), ALU.subtract),
                    S["kd"])
            M["kd", (b, q)] = M["pool"]

        TURN = bank(3)

        def score_bank(t):
            return bank((2, 7)[t % 2])

        def split_turned(stage, b, half, dst, *waits):
            act.wait(mark(stage + "_mm", (b, half)), *waits)
            M[stage + "_hi", (b, half)] = act.do(lambda e: e.copy(dst(0), TURN), S[stage + "_hi"])
            dve.wait(mark(stage + "_hi", (b, half)))
            M[stage + "_lo", (b, half)] = dve.do(lambda e: e.tensor_tensor(
                dst(1), TURN, f32(dst(0)), ALU.subtract), S[stage + "_lo"])
            M["turned"] = M[stage + "_lo", (b, half)]

        def turn(stage, b, half, src, *waits):
            pe.wait(M.get("turned"), *early, *waits)
            for c in range(4):
                m = pe.do(lambda e, c=c: e.transpose(TURN[:, c * P:(c + 1) * P], src(4 * half + c), ident[:]),
                          S[stage + "_mm"] if c == 3 else None)
            M[stage + "_mm", (b, half)] = m

        def turn_h(b, half):
            if in_range(b):
                turn("hT", b, half, lambda c: h_in[:, c * P:(c + 1) * P], M["h_early", b])

        def split_hT(b, half):
            if in_range(b):
                split_turned("hT", b, half, lambda part: hT[:, part, 4 * half:4 * half + 4, :].rearrange(
                    "p c n -> p (c n)"), mark("q_mm", b - 1))

        def turn_q(b, half):
            if in_range(b):
                turn("qT", b, half, lambda c: q_sb[:, c * P:(c + 1) * P], mark("q", b))

        def split_qT(b, half):
            if in_range(b):
                split_turned("qT", b, half, lambda part: qT[:, part, 4 * half:4 * half + 4, :].rearrange(
                    "p c n -> p (c n)"), mark("sc_mm", (b - 1) * UNITS + (half + 1) * GROUP - 1))

        def project(stage, b, left, weights, chunks):
            hi, lo = weights
            for c in chunks:
                for part, w in ((0, hi), (0, lo), (1, hi)):
                    for half in range(2):
                        first = c == 0 and part == 0 and w is hi
                        last = c == NC - 1 and part == 1
                        m = pe.do(lambda e, c=c, part=part, w=w, half=half, first=first, last=last: e.matmul(
                            bank(half), left[:, part, c, :], w[:, c, half * BANK:(half + 1) * BANK],
                            start=first, stop=last), S[stage] if half and part == 1 else None)
                M[stage, (b, c)] = m
            M[stage, b] = m

        def project_q(b, c):
            if in_range(b):
                pe.wait(mark("hT_lo", (b, c // 4)), mark("o", b - 3), (s_prep_lo, s_prep_lo.count),
                        mark("yT_lo", (B - 1, 1)))
                project("q_mm", b, hT, (wq_hi, wq_lo), (c,))

        def evacuate_q(b):
            if in_range(b):
                act.wait(mark("q_mm", b), mark("qT_mm", (b - 1, 1)))
                M["q", b] = act.do(lambda e: e.copy(q_sb[:], banks[0][:]), S["q"])

        def project_o(b, c):
            if in_range(b):
                pe.wait(mark("c_lo", (b, c // GROUP)), mark("q", b + 2), mark("o", b - 1), M["wo_in", c // 4])
                project("o_mm", b, cT, (wo_hi, wo_lo), (c,))

        def finish_out(b):
            if in_range(b):
                dve.wait(mark("o_mm", b), M["h_res", b])
                M["o", b] = dve.do(lambda e: e.tensor_tensor(
                    h_in[:], banks[0][:], h_in[:], ALU.add), S["o"])
                sp.wait(mark("o", b))
                M["out", b] = sp.do(lambda e: e.dma_start(out[b], h_in[:]), s_out, DMA)

        total = B * UNITS

        def scores(t):
            if not 0 <= t < total:
                return
            b, u = divmod(t, UNITS)
            q = u // GROUP
            pe.wait(mark("qT_lo", (b, q)), mark("kd", (b, q)), mark("exp", t - 2))
            for n, (part, kpart) in enumerate(((0, 0), (0, 1), (1, 0))):
                m = pe.do(lambda e, n=n, part=part, kpart=kpart: e.matmul(
                    score_bank(t), qT[:, part, u, :], k_diag[:, kpart, q, :, :].rearrange("p g t -> p (g t)"),
                    start=n == 0, stop=n == 2), S["sc_mm"] if n == 2 else None)
            M["sc_mm", t] = m

        def maxima(t):
            if not 0 <= t < total:
                return
            st_t = soft[t % 2]
            dve.wait(mark("sc_mm", t), mark("exp", t - 2))
            m = dve.do(lambda e: e.tensor_reduce(
                st_t[:, 0, :], score_bank(t).rearrange("p (g t) -> p g t", g=GQ), AX_X, ALU.max), S["max"])
            dve.wait(m)
            M["neg", t] = dve.do(lambda e: e.tensor_scalar(st_t[:, 1, :], st_t[:, 0, :], -SCORE1, None, ALU.mult),
                                 S["neg"])

        def exponents(t):
            if not 0 <= t < total:
                return
            st_t = soft[t % 2]
            act.wait(mark("neg", t), mark("pT_mm", t - 2), mark("norm", t - 2))
            for g in range(GQ):
                m = act.do(lambda e, g=g: e.activation(
                    prob[t % 2][:, g, :], score_bank(t)[:, g * P:(g + 1) * P], ACT.Exp,
                    bias=st_t[:, 1, g:g + 1], scale=SCORE1, accum_out=st_t[:, 2, g:g + 1]), S["exp"])
            M["exp", t] = m

        def normalise(t):
            if not 0 <= t < total:
                return
            st_t = soft[t % 2]
            dve.wait(mark("exp", t))
            m = dve.do(lambda e: e.reciprocal(st_t[:, 3, :], st_t[:, 2, :]), S["rec"])
            dve.wait(m)
            M["norm", t] = dve.do(lambda e: e.tensor_tensor(
                prob[t % 2][:], prob[t % 2][:], st_t[:, 3, :, None].to_broadcast([P, GQ, P]), ALU.mult), S["norm"])

        def turn_prob(t):
            if not 0 <= t < total:
                return
            pe.wait(mark("norm", t), mark("pT", t - 2))
            for g in range(GQ):
                m = pe.do(lambda e, g=g: e.transpose(
                    bank(4 + t % 2)[:, g * P:(g + 1) * P], prob[t % 2][:, g, :], ident[:]),
                    S["pT_mm"] if g == GQ - 1 else None)
            M["pT_mm", t] = m

        def evacuate_probT(t):
            if not 0 <= t < total:
                return
            quad, member = divmod(t, GROUP)
            act.wait(mark("pT_mm", t), mark("pv_mm", divmod(quad - 2, NQ)))
            M["pT", t] = act.do(lambda e: e.copy(
                probT[quad % 2][:, member, :, :].rearrange("p g n -> p (g n)"), bank(4 + t % 2)), S["pT"])

        def context(quad):
            if not 0 <= quad < B * NQ:
                return
            b, q = divmod(quad, NQ)
            pe.wait(mark("pT", quad * GROUP + GROUP - 1), M["v_in", (b, q)], mark("c_lo", divmod(quad - 1, NQ)))
            for g in range(GQ):
                m = pe.do(lambda e, g=g: e.matmul(
                    bank(6)[g * HD:(g + 1) * HD, :], v_in[:, q, g, :], probT[quad % 2][:, :, g, :],
                    start=True, stop=True), S["pv_mm"] if g == GQ - 1 else None)
            M["pv_mm", (b, q)] = m

        def split_context(quad):
            if not 0 <= quad < B * NQ:
                return
            b, q = divmod(quad, NQ)
            dst = [cT[:, part, q * GROUP:(q + 1) * GROUP, :].rearrange("p j n -> p (j n)") for part in range(2)]
            act.wait(mark("pv_mm", (b, q)), mark("o_mm", (b - 1, (q + 1) * GROUP - 1)))
            M["c_hi", (b, q)] = act.do(lambda e: e.copy(dst[0], bank(6)), S["c_hi"])
            dve.wait(mark("c_hi", (b, q)))
            M["c_lo", (b, q)] = dve.do(lambda e: e.tensor_tensor(dst[1], bank(6), f32(dst[0]), ALU.subtract),
                                       S["c_lo"])

        def slot(t):
            b, s = divmod(t, UNITS)
            scores(t)
            turn_prob(t - 2)
            quad_done = (t - GROUP - 2) // GROUP if (t - 2) % GROUP == 0 else None
            if quad_done is not None:
                context(quad_done)
            normalise(t - 1)
            maxima(t)
            evacuate_probT(t - 2)
            exponents(t)
            if quad_done is not None:
                split_context(quad_done)
            if s < 4:
                project_q(b + 1, 2 * s)
            else:
                project_o(b - 1, 2 * (s - 4))
            if s == 0:
                turn_q(b, 1)
                split_qT(b, 1)
                keys_diagonal(b, 1)
                load_k(b + 1)
            if s == 3:
                load_v(b, 1)
            if s in (4, 5):
                turn_h(b + 2, s - 4)
                split_hT(b + 2, s - 4)
                if s == 5:
                    load_h_res(b - 1)
            if s == 6:
                turn_q(b + 1, 0)
                split_qT(b + 1, 0)
            if s < 4:
                project_q(b + 1, 2 * s + 1)
                if s == 3:
                    evacuate_q(b + 1)
            else:
                project_o(b - 1, 2 * (s - 4) + 1)
                if s == 4:
                    keys_diagonal(b + 1, 0)
                if s == 7:
                    load_v(b + 1, 0)
                    finish_out(b - 1)
                    load_h_early(b + 3)

        sp.wait(*early)
        load_h_early(0)
        turn_k(B - 1)
        evacuate_kT(B - 1)
        slot(-12)
        partition_stats(B - 1)
        mean_product(B - 1)
        deviation(B - 1)
        slot(-11)
        var_product(B - 1)
        norm_factors(B - 1)
        norm_scale(B - 1)
        write_h(B - 1)
        for t in range(-10, 0):
            slot(t)
        late = [mark(n, B - 1) for n in ("kT_mm", "n1_mm", "mx_mm", "st2_mm", "mix_mm", "kT", "h", "gbi", "x_lo",
                                         "mix_lo")]
        late += [(s_prep_lo, s_prep_lo.count), (s_prep_hi, s_prep_hi.count)]
        late += [h_stored[B - 2], h_stored[B - 1], kv_stored[B - 2], kv_stored[B - 1], *o_stored]
        for lane in (pe, act, dve, pool, sp):
            lane.wait(*late)
        for r in range(2):
            for part, w in ((0, wo_hi), (1, wo_lo)):
                for c in range(4 * r, 4 * r + 4):
                    M["wo_in", r] = load(f32(w[:, c, :]), wo_dram[part][c], s_wo_in)
        for t in range(total + UNITS):
            slot(t)
        sp.wait(M["out", B - 1])

        with nc.Block() as block:
            @block.tensor
            def _(eng):
                pe.play(eng)

            @block.scalar
            def _(eng):
                act.play(eng)

            @block.vector
            def _(eng):
                dve.play(eng)

            @block.gpsimd
            def _(eng):
                pool.play(eng)

            @block.sync
            def _(eng):
                sp.play(eng)


_INS = ["x", "ctx_4096",
        "L0_xattn_Wq", "L0_xattn_bq", "L0_xattn_Wk", "L0_xattn_bk", "L0_xattn_Wv", "L0_xattn_bv",
        "L0_xattn_Wo", "L0_xattn_bo", "L0_xattn_gn_w", "L0_xattn_gn_b",
        "L1_xattn_Wq", "L1_xattn_Aq", "L1_xattn_Bq", "L1_xattn_Wk", "L1_xattn_Ak", "L1_xattn_Bk",
        "L1_xattn_Wv", "L1_xattn_Av", "L1_xattn_Bv", "L1_xattn_Wo", "L1_xattn_Ao", "L1_xattn_Bo"]


def kernel(**inputs):
    import numpy as np
    import concourse.bacc as bacc
    from concourse.bass_utils import run_bass_kernel_spmd

    nc = bacc.Bacc("TRN2", target_bir_lowering=False, num_devices=1)
    arrays, args = {}, []
    for name in _INS:
        a = np.ascontiguousarray(inputs[name])
        arrays[f"in_{name}"] = a
        args.append(nc.dram_tensor(f"in_{name}", a.shape, mybir.dt.from_np(a.dtype), kind="ExternalInput").ap())
    shape = arrays["in_x"].shape
    out = nc.dram_tensor("out_dram", shape, F32, kind="ExternalOutput").ap()
    xattn_two_layers(nc, *args, out)
    result = run_bass_kernel_spmd(nc, [arrays], core_ids=[0])
    return result.results[0]["out_dram"]
```

```python
from contextlib import ExitStack

import concourse.bass as bass
from concourse import mybir

F32 = mybir.dt.float32
F32R = mybir.dt.float32r
ALU = mybir.AluOpType
ACT = mybir.ActivationFunctionType
AX_X = mybir.AxisListType.X

P = 128
BANK = 512
DMA = 16


class Signal:

    def __init__(self, sem):
        self.sem, self.count = sem, 0

    def mark(self, step):
        self.count += step
        return self, self.count


class Lane:

    def __init__(self):
        self.steps, self.passed = [], {}

    def wait(self, *marks):
        for signal, count in (m for m in marks if m is not None):
            if self.passed.get(signal, 0) < count:
                self.passed[signal] = count
                self.steps.append(lambda eng, s=signal.sem, c=count: eng.wait_ge(s, c))

    def do(self, make, signal=None, step=1):
        if signal is None:
            self.steps.append(make)
            return None
        self.steps.append(lambda eng, s=signal.sem: make(eng).then_inc(s, step))
        return signal.mark(step)

    def play(self, eng):
        for step in self.steps:
            step(eng)


def xattn_two_layers(nc, x, ctx_4096, Wq0, bq0, Wk0, bk0, Wv0, bv0, Wo0, bo0, gn_w, gn_b,
                     Wq, Aq, Bq, Wk, Ak, Bk, Wv, Av, Bv, Wo, Ao, Bo, out):
    B, E, L = x.shape
    HID = Wq.shape[1]
    KV = Wk.shape[1]
    R = Aq.shape[1]
    NC = HID // P
    H0, D0 = 8, E // 8
    NH, HD = 32, HID // 32
    NKV = KV // HD
    GROUP = NH // NKV
    GQ = P // HD
    NQ = NKV // GQ
    UNITS = NQ * GROUP
    PAIRS = NH // 2
    LORA_SCALE = 32.0 / 16.0
    SCORE0 = float(E) ** -0.5
    SCORE1 = float(HD) ** -0.5
    EPS = 1e-5
    OFF_BLOCK = -1e30
    assert E == P and HID == 2 * BANK and 2 * KV == BANK and GQ * P == BANK and L == HID

    with ExitStack() as ctx:
        end = nc.sbuf_usable_end
        start = (nc.sbuf_base + 63) // 64 * 64
        at = [start]

        def sb(name, shape, dt=F32):
            size = 4
            for n in shape[1:]:
                size *= n
            a = at[0]
            at[0] = a + (size + 31) // 32 * 32
            assert at[0] <= end, (name, at[0], end)
            return nc.alloc_sbuf_tensor_at(name, shape, dt, offset=a)

        def signal(name):
            return Signal(ctx.enter_context(nc.semaphore(name)))

        def scratch(name, shape, dt=F32):
            return nc.dram_tensor(name, shape, dt, kind="Internal").ap()

        pe, act, dve, pool, sp = Lane(), Lane(), Lane(), Lane(), Lane()

        h_dram = scratch("h_dram", (B, P, HID))
        kT_dram = scratch("kT_dram", (B, P, KV // P * P))
        v_dram = scratch("v_dram", (B, P, KV))
        wo_dram = [scratch(f"wo_{s}_dram", (NC, P, HID)) for s in ("hi", "lo")]

        ident = sb("ident", [P, P])
        w_place = at[0]
        wq_hi = sb("wq_hi", [P, NC, HID], F32R)
        wq_lo = sb("wq_lo", [P, NC, HID], F32R)
        shared = at[0]

        wkv_hi = sb("wkv_hi", [P, NC, 2 * KV], F32R)
        wkv_lo = sb("wkv_lo", [P, NC, 2 * KV], F32R)
        y_in = [sb(f"y_in{i}", [P, L]) for i in range(2)]
        yT = [sb(f"yT{i}", [P, NC, 2, P], F32R) for i in range(2)]
        early_end = at[0]
        x_in = [sb(f"x_in{i}", [P, L]) for i in range(2)]
        x_hi = sb("x_hi", [P, L], F32R)
        x_lo = sb("x_lo", [P, L], F32R)
        h_out = [sb(f"h_out{i}", [P, L]) for i in range(2)]
        kv_sb = [sb(f"kv_sb{i}", [P, 2 * KV]) for i in range(2)]
        kT_sb = [sb(f"kT_sb{i}", [P, KV]) for i in range(2)]
        w_raw = [sb(f"w_raw{i}", [P, BANK]) for i in range(2)]
        o_split = [sb(f"o_split{i}", [P, 2, BANK], F32R) for i in range(2)]
        lora_cols = {"kv": 2 * KV, "q": HID, "o": HID}
        lora_aT = {m: sb(f"lora_aT_{m}", [P, HID], F32R) for m in lora_cols}
        lora_b = {m: sb(f"lora_b_{m}", [P, n], F32R) for m, n in lora_cols.items()}
        lora_a, lora_a3, lora_b3 = {}, {}, {}

        def lora_raw(m):
            lora_a[m] = sb(f"lora_a_{m}", [P, NC, 2 * R])
            lora_a3[m] = sb(f"lora_a3_{m}", [P, NC, P])
            lora_b3[m] = sb(f"lora_b3_{m}", [P, lora_cols[m]])

        ones_avg = sb("ones_avg", [P, P])
        w0T = sb("w0T", [P, 3, P])
        wv0 = sb("wv0", [P, P])
        bias_rows = sb("bias_rows", [1, 2, P])
        ones_row = sb("ones_row", [1, P])
        bqk = sb("bqk", [P, 2, P])
        score_bias = sb("score_bias", [P, P])
        columns = sb("columns", [P, 5])
        bq_col, bv_col, bo_col, gnw_col, gnb_col = (columns[:, i:i + 1] for i in range(5))
        bq_scaled = sb("bq_scaled", [P, 1])
        minus_half = sb("minus_half", [P, 1])
        y_sum = sb("y_sum", [P, 2])
        gram_mixed = sb("gram_mixed", [P, P])
        gram = sb("gram", [P, P])
        t1 = sb("t1", [P, P])
        s_bq = sb("s_bq", [P, P])
        att = sb("att", [P, P])
        n1 = sb("n1", [P, P])
        mix = sb("mix", [P, P])
        mix_split = sb("mix_split", [P, 2, P], F32R)
        att_stat = sb("att_stat", [P, 4])
        norm = sb("norm", [P, 16])
        bn = sb("bn", [P, 2, 6])

        lora_o_place = at[0]
        lora_raw("o")

        at[0] = w_place
        wkv_raw = sb("wkv_raw", [P, NC, 2 * KV])
        w0_raw = sb("w0_raw", [P, 3, P])
        for m in ("kv", "q"):
            lora_raw(m)
        assert at[0] <= shared

        at[0] = shared
        q_split = sb("q_split", [P, PAIRS, 2, 2 * HD], F32R)
        qT = sb("qT", [P, PAIRS, P], F32R)
        k_diag = sb("k_diag", [P, NQ, 2, 2, 2, P], F32R)
        k_in = sb("k_in", [P, NQ, 2, P])
        v_in = sb("v_in", [P, NQ, GQ, HD])
        wo_hi = sb("wo_hi", [P, NC, HID], F32R)
        early_wo = (early_end - (at[0] - 4 * NC * HID)) // (4 * HID)
        wo_lo = sb("wo_lo", [P, NC, HID], F32R)
        prob = [sb(f"prob{i}", [P, GQ, P]) for i in range(2)]
        probT = [sb(f"probT{i}", [P, GROUP, GQ, P]) for i in range(2)]
        cT = sb("cT", [P, 2, UNITS, P], F32R)
        soft = [sb(f"soft{i}", [P, 4, GQ]) for i in range(2)]
        assert at[0] <= lora_o_place
        at[0] = lora_o_place
        hT = sb("hT", [P, 2, NC, P], F32R)
        h_in = sb("h_in", [P, HID])

        banks = [ctx.enter_context(nc.psum_tensor(f"bank{i}", [P, 2 * BANK], F32)) for i in range(4)]

        def bank(i):
            return banks[i // 2][:, i % 2 * BANK:(i % 2 + 1) * BANK]

        def f32(ap):
            return ap.bitcast(F32)

        s_pool = signal("s_pool")
        s_pe0 = signal("s_pe0")
        s_act0 = signal("s_act0")
        s_dve0 = signal("s_dve0")

        lora_zero = {}

        def clear_lora(m):
            pool.do(lambda e: e.memset(lora_b3[m][:], 0.0))
            lora_zero[m] = pool.do(lambda e: e.memset(lora_a3[m][:], 0.0), s_pool)

        clear_lora("kv")
        ident_zero = pool.do(lambda e: e.memset(ident[:], 0.0), s_pool)
        mask_zero = pool.do(lambda e: e.memset(score_bias[:], 0.0), s_pool)
        pool.wait(ident_zero)
        ident_ok = pool.do(lambda e: e.affine_select(
            out=ident[:], in_=ident[:], compare_op=ALU.not_equal, fill=1.0, base=0,
            pattern=[[-1, P]], channel_multiplier=1), s_pool)
        mask = score_bias[:].rearrange("p (b e) -> p b e", b=H0)
        pool.wait(mask_zero)
        above = pool.do(lambda e: e.affine_select(
            out=mask, in_=mask, compare_op=ALU.is_ge, fill=OFF_BLOCK, base=0,
            pattern=[[-D0, H0], [0, D0]], channel_multiplier=1), s_pool)
        pool.wait(above)
        mask_ok = pool.do(lambda e: e.affine_select(
            out=mask, in_=mask, compare_op=ALU.is_ge, fill=OFF_BLOCK, base=D0 - 1,
            pattern=[[D0, H0], [0, D0]], channel_multiplier=-1), s_pool)
        ones_ok = pool.do(lambda e: e.memset(ones_row[:], 1.0), s_pool)
        pool.do(lambda e: e.memset(minus_half[:], -0.5), s_pool)
        avg_ok = pool.do(lambda e: e.memset(ones_avg[:], 1.0 / P), s_pool)
        clear_lora("q")
        clear_lora("o")

        def load(dst, src, sig):
            return sp.do(lambda e: e.dma_start(dst, src), sig, DMA)

        s_y = [signal(f"s_y{i}") for i in range(2)]
        s_x = [signal(f"s_x{i}") for i in range(2)]
        s_wraw = [signal(f"s_wraw{i}") for i in range(2)]
        s_w0 = signal("s_w0")

        factors = {"kv": ((Ak, 0, Bk, 0), (Av, R, Bv, KV)), "q": ((Aq, 0, Bq, 0),), "o": ((Ao, 0, Bo, 0),)}
        lora_loaded = {}

        lora_signal = {m: signal(f"s_lora_{m}") for m in lora_cols}

        def load_lora_a(m):
            for a, first, b, col in factors[m]:
                if m == "o":
                    rows = a.rearrange("(q g j d) r -> q g d j r", q=NQ, g=GQ, j=GROUP)
                    for q in range(NQ):
                        for g in range(GQ):
                            load(lora_a[m][g * HD:(g + 1) * HD, q * GROUP:(q + 1) * GROUP, first:first + R],
                                 rows[q, g], lora_signal[m])
                else:
                    load(lora_a[m][:, :, first:first + R], a.rearrange("(c p) r -> p c r", p=P),
                         lora_signal[m])

        def load_lora_b(m):
            sp.wait(lora_zero[m])
            for a, first, b, col in factors[m]:
                for q in range(3):
                    lora_loaded[m] = load(
                        lora_b3[m][32 * q + first:32 * q + first + R, col:col + b.shape[1]], b,
                        lora_signal[m])

        s_wkv = [signal(f"s_wkv{i}") for i in range(2)]
        wkv_loaded = [None, None]

        def load_wkv(i):
            chunks = slice(i * NC // 2, (i + 1) * NC // 2)
            load(wkv_raw[:, chunks, 0:KV], Wk.rearrange("(c p) n -> p c n", p=P)[:, chunks, :], s_wkv[i])
            wkv_loaded[i] = load(wkv_raw[:, chunks, KV:2 * KV],
                                 Wv.rearrange("(c p) n -> p c n", p=P)[:, chunks, :], s_wkv[i])

        load_lora_a("kv")
        y_loaded = {0: load(y_in[0][:], ctx_4096[0], s_y[0])}
        load_lora_b("kv")
        load_wkv(0)
        load_wkv(1)
        for dst, src in ((w0_raw[:, 0, :], Wq0), (w0_raw[:, 1, :], Wk0), (w0_raw[:, 2, :], Wo0), (wv0[:], Wv0)):
            load(dst, src, s_w0)
        for row, src in ((0, bq0), (1, bk0)):
            load(bias_rows[:, row, :], src.rearrange("(a n) -> a n", a=1), s_w0)
        for col, src in ((bq_col, bq0), (bv_col, bv0), (bo_col, bo0), (gnw_col, gn_w), (gnb_col, gn_b)):
            w0_loaded = load(col, src.rearrange("(n a) -> n a", a=1), s_w0)

        small_free = [None, None]
        small_turn = [0]

        def small_bank():
            i = small_turn[0] % 2
            small_turn[0] += 1
            pe.wait(small_free[i])
            return i, bank(6 + i)

        lora_ready = {}
        M = {}

        def in_turn(lane, make, sig):
            if lane is not pool:
                return lane.do(make, sig)
            pool.wait(M.get("pool"))
            M["pool"] = pool.do(make, sig)
            return M["pool"]

        def stack_lora(m, lane, signal_of):
            used = R * len(factors[m])
            lane.wait(lora_loaded[m], lora_zero[m])
            for q in range(3):
                a3_ok = in_turn(lane, lambda e, q=q: e.tensor_scalar(
                    lora_a3[m][:, :, 32 * q:32 * q + used], lora_a[m][:, :, 0:used], 1.0, None, ALU.mult),
                    signal_of)
            hi = in_turn(lane, lambda e: e.tensor_scalar(lora_b[m][:], lora_b3[m][:], 1.0, None, ALU.mult),
                         signal_of)
            lane.wait(hi)
            b_ok = in_turn(lane, lambda e: e.tensor_tensor(
                lora_b[m][64:96, :], lora_b3[m][64:96, :], f32(lora_b[m][64:96, :]), ALU.subtract), signal_of)
            pe.wait(a3_ok, ident_ok)
            for half in range(2):
                i, ps = small_bank()
                for c in range(4):
                    turned = pe.do(lambda e, ps=ps, half=half, c=c: e.transpose(
                        ps[:, c * P:(c + 1) * P], lora_a3[m][:, 4 * half + c, :], ident[:]), s_pe0)
                dst = lora_aT[m][:, half * BANK:(half + 1) * BANK]
                act.wait(turned)
                hi = act.do(lambda e, dst=dst, ps=ps: e.copy(dst, ps), s_act0)
                dve.wait(hi)
                small_free[i] = aT_ok = dve.do(lambda e, dst=dst, ps=ps: e.tensor_tensor(
                    dst[32:64, :], ps[32:64, :], f32(dst[32:64, :]), ALU.subtract), s_dve0)
            lora_ready[m] = (b_ok, aT_ok)

        def turn_layer0():
            pe.wait(w0_loaded, ident_ok, ones_ok)
            for i in range(3):
                turned = pe.do(lambda e, i=i: e.transpose(
                    bank(4)[:, i * P:(i + 1) * P], w0_raw[:, i, :], ident[:]), s_pe0)
            for i in range(2):
                spread = pe.do(lambda e, i=i: e.matmul(bank(5)[:, i * P:(i + 1) * P], ones_row[:],
                                                       bias_rows[:, i, :], start=True, stop=True), s_pe0)
            act.wait(turned)
            w0T_ok = act.do(lambda e: e.copy(w0T[:].rearrange("p a b -> p (a b)"), bank(4)[:, 0:3 * P]), s_act0)
            act.wait(spread)
            bqk_ok = act.do(lambda e: e.copy(bqk[:].rearrange("p a b -> p (a b)"), bank(5)[:, 0:2 * P]), s_act0)
            return w0T_ok, bqk_ok

        def bias_scores():
            dve.wait(bqk_ok, mask_ok, w0_loaded)
            scaled = dve.do(lambda e: e.tensor_scalar(bq_scaled[:], bq_col, SCORE0 * L, None, ALU.mult), s_dve0)
            dve.wait(scaled)
            return dve.do(lambda e: e.scalar_tensor_tensor(
                score_bias[:], bqk[:, 1, :], bq_scaled[:], score_bias[:], ALU.mult, ALU.add), s_dve0)

        wqT0, wkT0, woT0 = (w0T[:, i, :] for i in range(3))

        def mark(stage, b):
            return M.get((stage, b))

        s_prep = signal("s_prep")
        s_prep_w = signal("s_prep_w")
        s_prep_hi = signal("s_prep_hi")
        s_prep_lo = signal("s_prep_lo")
        s_prep_lo_dve = signal("s_prep_lo_dve")
        s_wo_out = [signal(f"s_wo_out{i}") for i in range(2)]
        raw_free = [None, None]
        raw_loaded = {}
        o_stored = [None, None]
        units = [("kv", c, 0) for c in range(NC)]
        units += [(m, c, half) for m in ("q", "o") for c in range(NC) for half in range(2)]

        def raw_piece(n):
            return wkv_raw[:, units[n][1], :] if units[n][0] == "kv" else w_raw[n % 2][:]

        def load_raw(n):
            if n >= len(units):
                return
            m, c, half = units[n]
            i = n % 2
            sp.wait(raw_free[i])
            columns_of = slice(half * BANK, (half + 1) * BANK)
            if m == "q":
                raw_loaded[n] = load(w_raw[i][:], Wq[c * P:(c + 1) * P, columns_of], s_wraw[i])
            else:
                rows = Wo.rearrange("(q g j d) n -> q j g d n", q=NQ, g=GQ, j=GROUP)[c // GROUP, c % GROUP]
                for g in range(GQ):
                    raw_loaded[n] = load(w_raw[i][g * HD:(g + 1) * HD, :], rows[g, :, columns_of], s_wraw[i])

        prep_at = {}

        def prep_product(n):
            m, c, half = units[n]
            i, ps = small_bank()
            pe.wait(*lora_ready[m])
            prep_at[n] = i, pe.do(lambda e: e.matmul(
                ps, lora_aT[m][:, c * P:(c + 1) * P], lora_b[m][:, half * BANK:(half + 1) * BANK],
                start=True, stop=True), s_prep)

        def prep_merge(n):
            i, product = prep_at[n]
            raw = raw_piece(n)
            dve.wait(product, wkv_loaded[units[n][1] // (NC // 2)] if units[n][0] == "kv" else raw_loaded[n])
            small_free[i] = dve.do(lambda e: e.scalar_tensor_tensor(
                raw, bank(6 + i), LORA_SCALE, raw, ALU.mult, ALU.add), s_prep_w)
            return small_free[i]

        def prep_parts(n):
            m, c, half = units[n]
            raw = raw_piece(n)
            if m == "kv":
                return raw, wkv_hi[:, c, :], wkv_lo[:, c, :]
            if m == "q":
                hi, lo = (w[:, c, half * BANK:(half + 1) * BANK].rearrange(
                    "p (j g d) -> p g j d", g=GQ, j=GROUP) for w in (wq_hi, wq_lo))
                return raw.rearrange("p (g j d) -> p g j d", g=GQ, j=GROUP), hi, lo
            return raw, o_split[n % 2][:, 0, :], o_split[n % 2][:, 1, :]

        def prep_round(n, merged):
            m = units[n][0]
            raw, hi, lo = prep_parts(n)
            act.wait(merged)
            if m == "q":
                act.wait(*lora_ready["q"], w0T_ok, *wkv_ok)
            if m == "o":
                act.wait(o_stored[n % 2])
            return act.do(lambda e: e.copy(hi, raw), s_prep_hi)

        def prep_rest(n, rounded, lane, sig):
            m, c, half = units[n]
            raw, hi, lo = prep_parts(n)
            lane.wait(rounded)
            lo_ok = in_turn(lane, lambda e: e.tensor_tensor(lo, raw, f32(hi), ALU.subtract), sig)
            if m != "kv":
                raw_free[n % 2] = lo_ok
            if m == "o":
                sp.wait(lo_ok)
                for part in range(2):
                    o_stored[n % 2] = sp.do(lambda e, part=part: e.dma_start(
                        wo_dram[part][c, :, half * BANK:(half + 1) * BANK], f32(o_split[n % 2][:, part, :])),
                        s_wo_out[n % 2], DMA)
            return lo_ok

        wkv_ok = []
        wq_ok = []
        next_unit = [NC]

        names_a = ("yT_mm", "yT_hi", "yT_lo", "ysum", "gram_mm", "gram_m", "gram_h", "gram_turn", "gram",
                   "t1_mm", "t1", "sbq", "s_mm", "s_sb", "s_max", "s_neg", "s_exp", "s_rec", "att", "n1_mm",
                   "n1", "mix_mm", "mix", "mix_hi", "mix_lo", "xbias", "x_hi", "x_lo", "mx_mm", "bn", "agg", "st",
                   "st1_mm", "dev", "nm", "st2", "st2_mm", "ve", "pow", "gsc", "gbi", "h", "kv_mm",
                   "kv", "kT_mm", "kT")
        S = {n: signal("a_" + n) for n in names_a}
        s_h_out = [signal(f"s_h_out{i}") for i in range(2)]
        s_kv_out = [signal(f"s_kv_out{i}") for i in range(2)]

        def load_y(b):
            if 0 < b < B:
                sp.wait(mark("yT_mm", (b - 2, 1)), mark("ysum", b - 2))
                y_loaded[b] = load(y_in[b % 2][:], ctx_4096[b], s_y[b % 2])

        x_loaded = {}

        def load_x(b):
            if b < B:
                sp.wait(mark("x_hi", b - 2), mark("x_lo", b - 2))
                x_loaded[b] = load(x_in[b % 2][:], x[b], s_x[b % 2])

        def turn_y(b):
            if b >= B:
                return
            pe.wait(y_loaded[b], ident_ok, mark("yT_lo", (b - 1, 1)))
            for c in range(NC):
                m = pe.do(lambda e, c=c: e.transpose(
                    banks[0][:, c * P:(c + 1) * P], y_in[b % 2][:, c * P:(c + 1) * P], ident[:]),
                    S["yT_mm"] if c % 4 == 3 else None)
                M["yT_mm", (b, c // 4)] = m

        def yT_part(b, half, part):
            return (bank(half).rearrange("p (c n) -> p c n", c=4),
                    yT[b % 2][:, 4 * half:4 * half + 4, part, :])

        def round_yT(b, half):
            if b >= B:
                return
            src, hi = yT_part(b, half, 0)
            act.wait(mark("yT_mm", (b, half)), mark("kv_mm", b - 2), mark("gram_mm", b - 2))
            M["yT_hi", (b, half)] = act.do(lambda e: e.copy(hi, src), S["yT_hi"])

        def rest_yT(b, half):
            if b >= B:
                return
            src, hi = yT_part(b, half, 0)
            lo = yT_part(b, half, 1)[1]
            dve.wait(mark("yT_hi", (b, half)))
            M["yT_lo", (b, half)] = dve.do(lambda e: e.tensor_tensor(lo, src, f32(hi), ALU.subtract), S["yT_lo"])

        def kv_products(b, chunks):
            pe.wait(mark("kv", b - 1))
            for c in chunks:
                pe.wait(mark("yT_lo", (b, c // 4)), wkv_ok[c])
                for part, w in ((0, wkv_hi), (0, wkv_lo), (1, wkv_hi)):
                    first = c == 0 and part == 0 and w is wkv_hi
                    last = c == NC - 1 and part == 1
                    m = pe.do(lambda e, c=c, part=part, w=w, first=first, last=last: e.matmul(
                        bank(2), yT[b % 2][:, c, part, :], w[:, c, :], start=first, stop=last),
                        S["kv_mm"] if last else None)
            M["kv_mm", b] = m

        def sum_y(b):
            if b >= B:
                return
            dve.wait(y_loaded[b], mark("t1", b - 2), mark("sbq", b - 2))
            M["ysum", b] = dve.do(lambda e: e.tensor_reduce(
                y_sum[:, b % 2:b % 2 + 1], y_in[b % 2][:], AX_X, ALU.add), S["ysum"])

        def gram_products(b):
            pe.wait(mark("gram_m", b - 1), mark("gram_h", b - 1))
            for c in range(NC):
                pe.wait(mark("yT_lo", (b, c // 4)))
                m = pe.do(lambda e, c=c: e.matmul(
                    bank(3)[:, 0:2 * P], yT[b % 2][:, c, 0, :], yT[b % 2][:, c, :, :],
                    start=c == 0, stop=c == NC - 1), S["gram_mm"] if c == NC - 1 else None)
            M["gram_mm", b] = m

        def begin_gram(b):
            act.wait(mark("gram_mm", b), mark("gram_turn", b - 1), mark("gram_h", b - 1))
            M["gram_m", b] = act.do(lambda e: e.copy(gram_mixed[:], bank(3)[:, P:2 * P]), S["gram_m"])
            dve.wait(mark("gram_m", b), mark("t1_mm", b - 1))
            M["gram_h", b] = dve.do(lambda e: e.tensor_tensor(
                gram[:], bank(3)[:, 0:P], gram_mixed[:], ALU.add), S["gram_h"])

        def turn_gram(b):
            i, ps = small_bank()
            pe.wait(mark("gram_m", b))
            M["gram_turn", b] = pe.do(lambda e: e.transpose(ps[:, 0:P], gram_mixed[:], ident[:]), S["gram_turn"])
            held["gram", b] = i

        def finish_gram(b):
            i = held["gram", b]
            dve.wait(mark("gram_turn", b), mark("gram_h", b))
            small_free[i] = M["gram", b] = dve.do(lambda e: e.tensor_tensor(
                gram[:], bank(6 + i)[:, 0:P], gram[:], ALU.add), S["gram"])

        held = {}

        def small_product(stage, b, lhsT, rhs, *waits):
            i, ps = small_bank()
            pe.wait(*waits)
            M[stage, b] = pe.do(lambda e: e.matmul(ps[:, 0:rhs.shape[1]], lhsT, rhs, start=True, stop=True),
                                S[stage])
            return i

        def t1_product(b):
            held["t1", b] = small_product("t1_mm", b, gram[:], wkT0, mark("gram", b), w0T_ok)

        def weigh_bias(b):
            dve.wait(mark("ysum", b), mark("s_mm", b - 1), bqk_ok)
            M["sbq", b] = dve.do(lambda e: e.tensor_scalar(
                s_bq[:], bqk[:, 0, :], y_sum[:, b % 2:b % 2 + 1], None, ALU.mult), S["sbq"])

        def evacuate_t1(b):
            i = held["t1", b]
            dve.wait(mark("t1_mm", b), mark("ysum", b), mark("s_mm", b - 1), bqk_ok)
            small_free[i] = M["t1", b] = dve.do(lambda e: e.scalar_tensor_tensor(
                t1[:], bqk[:, 1, :], y_sum[:, b % 2:b % 2 + 1], bank(6 + i)[:, 0:P], ALU.mult, ALU.add), S["t1"])

        def score_product(b):
            i, ps = small_bank()
            pe.wait(mark("t1", b), mark("sbq", b))
            pe.do(lambda e: e.matmul(ps[:, 0:P], wqT0, t1[:], start=True, stop=False))
            M["s_mm", b] = pe.do(lambda e: e.matmul(ps[:, 0:P], s_bq[:], wkT0, start=False, stop=True), S["s_mm"])
            held["s", b] = i

        def softmax0_begin(b):
            i = held["s", b]
            dve.wait(mark("s_mm", b), score_bias_ok, mark("n1_mm", b - 1))
            small_free[i] = dve.do(lambda e: e.scalar_tensor_tensor(
                att[:], bank(6 + i)[:, 0:P], SCORE0, score_bias[:], ALU.mult, ALU.add), S["s_sb"])
            dve.wait(small_free[i])
            top = dve.do(lambda e: e.tensor_reduce(att_stat[:, 0:1], att[:], AX_X, ALU.max), S["s_max"])
            dve.wait(top)
            neg = dve.do(lambda e: e.tensor_scalar(att_stat[:, 1:2], att_stat[:, 0:1], -1.0, None, ALU.mult),
                         S["s_neg"])
            act.wait(neg)
            M["s_exp", b] = act.do(lambda e: e.activation(
                att[:], att[:], ACT.Exp, bias=att_stat[:, 1:2], scale=1.0, accum_out=att_stat[:, 2:3]),
                S["s_exp"])

        def softmax0_end(b):
            dve.wait(mark("s_exp", b))
            inverse = dve.do(lambda e: e.reciprocal(att_stat[:, 3:4], att_stat[:, 2:3]), S["s_rec"])
            dve.wait(inverse)
            M["att", b] = dve.do(lambda e: e.tensor_scalar(att[:], att[:], att_stat[:, 3:4], None, ALU.mult),
                                 S["att"])

        def n1_product(b):
            held["n1", b] = small_product("n1_mm", b, att[:], woT0, mark("att", b))

        def evacuate_n1(b):
            i = held["n1", b]
            act.wait(mark("n1_mm", b), mark("mix_mm", b - 1))
            small_free[i] = M["n1", b] = act.do(lambda e: e.copy(n1[:], bank(6 + i)[:, 0:P]), S["n1"])

        def mix_product(b):
            i, ps = small_bank()
            pe.wait(mark("n1", b))
            pe.do(lambda e: e.matmul(ps[:, 0:P], wv0[:], n1[:], start=True, stop=True))
            M["mix_mm", b] = pe.do(lambda e: e.matmul(ps[:, P:P + 1], n1[:], bv_col, start=True, stop=True),
                                   S["mix_mm"])
            held["mix", b] = i

        xbias, mv, st, dev, nm, st2, ve, rstd, gsc, gbi = (
            norm[:, 0:1], norm[:, 1:3], norm[:, 3:4], norm[:, 4:5], norm[:, 5:6], norm[:, 6:7],
            norm[:, 7:8], norm[:, 8:9], norm[:, 9:10], norm[:, 10:11])

        def split_mix(b):
            i = held["mix", b]
            dve.wait(mark("mix_mm", b), mark("mx_mm", b - 1))
            M["mix", b] = dve.do(lambda e: e.tensor_tensor(mix[:], bank(6 + i)[:, 0:P], ident[:], ALU.add), S["mix"])
            small_free[i] = M["xbias", b] = dve.do(lambda e: e.tensor_tensor(
                xbias, bank(6 + i)[:, P:P + 1], bo_col, ALU.add), S["xbias"])
            dve.wait(mark("mix", b))
            M["mix_hi", b] = dve.do(lambda e: e.tensor_copy(mix_split[:, 0, :], mix[:]), S["mix_hi"])
            dve.wait(mark("mix_hi", b))
            M["mix_lo", b] = dve.do(lambda e: e.tensor_tensor(
                mix_split[:, 1, :], mix[:], f32(mix_split[:, 0, :]), ALU.subtract), S["mix_lo"])

        def split_x(b):
            if not 0 <= b < B:
                return
            act.wait(x_loaded[b], mark("mx_mm", b - 1))
            M["x_hi", b] = act.do(lambda e: e.copy(x_hi[:], x_in[b % 2][:]), S["x_hi"])
            pool.wait(mark("x_hi", b))
            M["x_lo", b] = in_turn(pool, lambda e: e.tensor_tensor(
                x_lo[:], x_in[b % 2][:], f32(x_hi[:]), ALU.subtract), S["x_lo"])

        def mixed_x(b):
            pe.wait(mark("mix_lo", b), mark("x_lo", b), mark("h", b - 1), bqk_ok)
            for part, xs in ((0, x_hi), (0, x_lo), (1, x_hi)):
                for half in range(2):
                    first, last = part == 0 and xs is x_hi, part == 1
                    m = pe.do(lambda e, part=part, xs=xs, half=half, first=first, last=last: e.matmul(
                        bank(4 + half), mix_split[:, part, :], xs[:, half * BANK:(half + 1) * BANK],
                        start=first, stop=last), S["mx_mm"] if last and half else None)
            M["mx_mm", b] = m

        def partition_stats(b):
            dve.wait(mark("mx_mm", b), mark("xbias", b))
            for half in range(2):
                m = dve.do(lambda e, half=half: e.bn_stats(bn[:, half, :], bank(4 + half)), S["bn"])
            dve.wait(m)
            m = dve.do(lambda e: e.bn_aggr(mv, bn[:].rearrange("p a b -> p (a b)")), S["agg"])
            dve.wait(m)
            M["st", b] = dve.do(lambda e: e.tensor_tensor(st, mv[:, 0:1], xbias, ALU.add), S["st"])

        def mean_product(b):
            held["st1", b] = small_product("st1_mm", b, ones_avg[:], st, mark("st", b), avg_ok)

        def deviation(b):
            i = held["st1", b]
            mean = bank(6 + i)[:, 0:1]
            dve.wait(mark("st1_mm", b))
            m = dve.do(lambda e: e.tensor_tensor(dev, st, mean, ALU.subtract), S["dev"])
            small_free[i] = M["nm", b] = dve.do(lambda e: e.tensor_tensor(nm, xbias, mean, ALU.subtract), S["nm"])
            dve.wait(m)
            M["st2", b] = dve.do(lambda e: e.scalar_tensor_tensor(st2, dev, dev, mv[:, 1:2], ALU.mult, ALU.add),
                                 S["st2"])

        def var_product(b):
            held["st2", b] = small_product("st2_mm", b, ones_avg[:], st2, mark("st2", b))

        def norm_factors(b):
            i = held["st2", b]
            dve.wait(mark("st2_mm", b), mark("h", b - 1))
            small_free[i] = m = dve.do(lambda e: e.tensor_scalar(ve, bank(6 + i)[:, 0:1], EPS, None, ALU.add), S["ve"])
            pool.wait(m)
            m = in_turn(pool, lambda e: e.tensor_tensor(rstd, ve, minus_half[:], ALU.pow), S["pow"])
            M["pow", b] = m

        def norm_scale(b):
            dve.wait(mark("pow", b), w0_loaded)
            m = dve.do(lambda e: e.tensor_tensor(gsc, rstd, gnw_col, ALU.mult), S["gsc"])
            dve.wait(m, mark("nm", b))
            M["gbi", b] = dve.do(lambda e: e.scalar_tensor_tensor(gbi, nm, gsc, gnb_col, ALU.mult, ALU.add), S["gbi"])

        h_stored = {}
        kv_stored = {}

        def write_h(b):
            act.wait(mark("gbi", b), mark("mx_mm", b), h_stored.get(b - 2))
            M["h", b] = act.do(lambda e: e.activation(
                h_out[b % 2][:], banks[2][:], ACT.Identity, bias=gbi, scale=gsc), S["h"])
            sp.wait(mark("h", b))
            h_stored[b] = sp.do(lambda e: e.dma_start(h_dram[b], h_out[b % 2][:]), s_h_out[b % 2], DMA)

        def evacuate_kv(b):
            act.wait(mark("kv_mm", b), kv_stored.get(b - 2), mark("kT_mm", b - 2))
            M["kv", b] = act.do(lambda e: e.copy(kv_sb[b % 2][:], bank(2)), S["kv"])

        def turn_k(b):
            i, ps = small_bank()
            pe.wait(mark("kv", b))
            for c in range(KV // P):
                m = pe.do(lambda e, c=c: e.transpose(
                    ps[:, c * P:(c + 1) * P], kv_sb[b % 2][:, c * P:(c + 1) * P], ident[:]),
                    S["kT_mm"] if c == KV // P - 1 else None)
            M["kT_mm", b] = m
            held["kT", b] = i

        def evacuate_kT(b):
            i = held["kT", b]
            act.wait(mark("kT_mm", b), kv_stored.get(b - 2))
            small_free[i] = M["kT", b] = act.do(lambda e: e.copy(kT_sb[b % 2][:], bank(6 + i)[:, 0:KV]), S["kT"])
            sp.wait(mark("kv", b), mark("kT", b))
            sp.do(lambda e: e.dma_start(v_dram[b], kv_sb[b % 2][:, KV:2 * KV]), s_kv_out[b % 2], DMA)
            kv_stored[b] = sp.do(lambda e: e.dma_start(kT_dram[b], kT_sb[b % 2][:]), s_kv_out[b % 2], DMA)

        load_x(0)
        load_y(1)
        load_lora_a("q")
        load_lora_b("q")
        load_raw(NC)
        load_raw(NC + 1)
        load_lora_a("o")
        load_lora_b("o")
        turn_y(0)
        stack_lora("kv", dve, s_dve0)
        for half in range(2):
            round_yT(0, half)
            rest_yT(0, half)
        prep_product(0)
        rounded = prep_round(0, prep_merge(0))
        for n in range(NC):
            if n + 1 < NC:
                prep_product(n + 1)
                merged = prep_merge(n + 1)
            if n == 0:
                gram_products(0)
            if n == 1:
                begin_gram(0)
            if n == 4:
                w0T_ok, bqk_ok = turn_layer0()
            wkv_ok.append(prep_rest(n, rounded, *((dve, s_prep_lo_dve) if n % 2 else (pool, s_prep_lo))))
            if n + 1 < NC:
                rounded = prep_round(n + 1, merged)
        sum_y(0)
        score_bias_ok = bias_scores()

        PIECES_LATE = len(units) - NC - (B - 1)
        UNIT_EXTRA = 3
        assert PIECES_LATE == 1
        merged_unit = []

        def finish_prepare():
            while merged_unit:
                n, merged = merged_unit.pop()
                lo_ok = prep_rest(n, prep_round(n, merged), pool, s_prep_lo)
                if units[n][0] == "q":
                    wq_ok[:] = [lo_ok]
                load_raw(n + 2)

        def sequence_a(b):
            old = b > 0
            if old:
                gram_products(b)
                partition_stats(b - 1)
            split_x(b)
            if old:
                begin_gram(b)
            load_y(b + 2)
            load_x(b + 1)
            if b == B - 2:
                sp.wait(*lora_ready["o"])
                act.wait(*lora_ready["o"])
                load_h_early(0)
            finish_prepare()
            kv_products(b, (0,))
            turn_gram(b)
            finish_gram(b)
            weigh_bias(b)
            kv_products(b, (1,))
            if old:
                mean_product(b - 1)
                deviation(b - 1)
            t1_product(b)
            evacuate_t1(b)
            kv_products(b, (2,))
            if old:
                var_product(b - 1)
                norm_factors(b - 1)
            score_product(b)
            turn_y(b + 1)
            round_yT(b + 1, 0)
            softmax0_begin(b)
            rest_yT(b + 1, 0)
            round_yT(b + 1, 1)
            softmax0_end(b)
            rest_yT(b + 1, 1)
            if old:
                norm_scale(b - 1)
            sum_y(b + 1)
            kv_products(b, (3, 4, 5))
            if b == B - 1:
                turn_h(0, 0)
                split_hT(0, 0)
            n1_product(b)
            evacuate_n1(b)
            if old:
                write_h(b - 1)
            kv_products(b, (6,))
            mix_product(b)
            split_mix(b)
            kv_products(b, (7,))
            evacuate_kv(b)
            if old:
                turn_k(b - 1)
                evacuate_kT(b - 1)
            if b < 2:
                stack_lora(("q", "o")[b], pool, s_pool)
            for n in range(next_unit[0], next_unit[0] + (0 if b == 0 else 1 + PIECES_LATE * (b == UNIT_EXTRA))):
                finish_prepare()
                prep_product(n)
                merged_unit.append((n, prep_merge(n)))
                next_unit[0] = n + 1
            if b == B - 1:
                turn_h(0, 1)
                split_hT(0, 1)
            mixed_x(b)

        s_wo_in = [signal(f"s_wo_in{i}") for i in range(2)]
        s_he = signal("s_he")
        s_hr = signal("s_hr")
        s_k = signal("s_k")
        s_v = [signal(f"s_v{q}") for q in range(NQ)]
        s_out = signal("s_out")
        names_b = ("kd", "hT_mm", "hT_hi", "hT_lo", "q_mm", "q_hi", "q_lo", "qT_mm", "qT", "sc_mm",
                   "max", "neg", "exp", "rec", "norm", "pT_mm", "pT", "pv_mm", "c_hi", "c_lo",
                   "o_mm", "o")
        S.update({n: signal("b_" + n) for n in names_b})

        def in_range(b):
            return 0 <= b < B

        def load_h_early(b):
            if in_range(b):
                sp.wait(h_stored[b], mark("hT_mm", (b - 1, 1)), mark("out", b - 4))
                M["h_early", b] = load(h_in[:], h_dram[b], s_he)

        def load_h_res(b):
            if in_range(b):
                sp.wait(mark("hT_mm", (min(b + 3, B - 1), 1)), mark("out", b - 1))
                M["h_res", b] = load(h_in[:], h_dram[b], s_hr)

        def load_k(b):
            if in_range(b):
                sp.wait(kv_stored[b], mark("kd", (b - 1, NQ - 1)))
                for pair in range(2):
                    rows = kT_dram[b][pair * 2 * HD:(pair + 1) * 2 * HD, :].rearrange("p (q t) -> p q t", q=NQ)
                    for part in range(2):
                        M["k_in", b] = load(k_in[part * 2 * HD:(part + 1) * 2 * HD, :, pair, :], rows, s_k)

        def load_v(b, q):
            if in_range(b):
                sp.wait(kv_stored[b], mark("pv_mm", (b - 1, q)))
                M["v_in", (b, q)] = load(v_in[:, q, :, :], v_dram[b][:, q * P:(q + 1) * P].rearrange(
                    "p (g d) -> p g d", g=GQ), s_v[q])

        def keys_diagonal(b, q):
            if not in_range(b):
                return
            pool.wait(M["k_in", b], mark("sc_mm", (b - 1) * UNITS + (q + 1) * GROUP - 1))
            for block in range(P // HD):
                rows, g = slice(block * HD, (block + 1) * HD), block % 2
                in_turn(pool, lambda e, rows=rows, g=g: e.tensor_scalar(
                    k_diag[rows, q, :, 0, g, :], k_in[rows, q, :, :], 1.0, None, ALU.mult), S["kd"])
                if block < 2:
                    in_turn(pool, lambda e, rows=rows, g=g: e.tensor_tensor(
                        k_diag[rows, q, :, 1, g, :], k_in[rows, q, :, :], f32(k_diag[rows, q, :, 0, g, :]),
                        ALU.subtract), S["kd"])
            M["kd", (b, q)] = M["pool"]

        TURN = bank(3)

        def score_bank(t):
            return bank((2, 7)[t % 2])

        def split_turned(stage, b, half, dst, *waits):
            act.wait(mark(stage + "_mm", (b, half)), *waits)
            M[stage + "_hi", (b, half)] = act.do(lambda e: e.copy(dst(0), TURN), S[stage + "_hi"])
            dve.wait(mark(stage + "_hi", (b, half)))
            M[stage + "_lo", (b, half)] = dve.do(lambda e: e.tensor_tensor(
                dst(1), TURN, f32(dst(0)), ALU.subtract), S[stage + "_lo"])
            M["turned"] = M[stage + "_lo", (b, half)]

        def turn(stage, b, half, src, *waits):
            pe.wait(M.get("turned"), mark("gram_m", B - 1), mark("gram_h", B - 1), *waits)
            for c in range(4):
                m = pe.do(lambda e, c=c: e.transpose(TURN[:, c * P:(c + 1) * P], src(4 * half + c), ident[:]),
                          S[stage + "_mm"] if c == 3 else None)
            M[stage + "_mm", (b, half)] = m

        def turn_h(b, half):
            if in_range(b):
                turn("hT", b, half, lambda c: h_in[:, c * P:(c + 1) * P], M["h_early", b])

        def split_hT(b, half):
            if in_range(b):
                split_turned("hT", b, half, lambda part: hT[:, part, 4 * half:4 * half + 4, :].rearrange(
                    "p c n -> p (c n)"), mark("q_mm", b - 1))

        def turn_q(b, group):
            if not in_range(b):
                return
            pe.wait(M.get("turned"), mark("q_lo", (b, group // 2)))
            for c in range(4):
                m = pe.do(lambda e, c=c: e.transpose(
                    TURN[:, c * P:(c + 1) * P],
                    f32(q_split[:, 4 * group + c, :, :]).rearrange("p a n -> p (a n)"), ident[:]),
                    S["qT_mm"] if c == 3 else None)
            M["qT_mm", (b, group)] = m

        def evacuate_qT(b, group):
            if not in_range(b):
                return
            act.wait(mark("qT_mm", (b, group)), mark("sc_mm", (b - 1) * UNITS + 2 * group + 1))
            M["turned"] = M["qT", (b, group)] = act.do(lambda e: e.copy(
                qT[:, 4 * group:4 * group + 4, :].rearrange("p c n -> p (c n)"), TURN), S["qT"])

        def project(stage, b, left, weights, chunks, free):
            hi, lo = weights
            for c in chunks:
                for half in range(2):
                    if c == 0:
                        pe.wait(*free[half])
                    for part, w in ((0, hi), (0, lo), (1, hi)):
                        first = c == 0 and part == 0 and w is hi
                        last = c == NC - 1 and part == 1
                        m = pe.do(lambda e, c=c, part=part, w=w, half=half, first=first, last=last: e.matmul(
                            bank(half), left[:, part, c, :], w[:, c, half * BANK:(half + 1) * BANK],
                            start=first, stop=last), S[stage] if part == 1 else None)
                    M[stage, (b, "half", half)] = m
                M[stage, (b, c)] = m
            M[stage, b] = m

        def project_q(b, c):
            if in_range(b):
                pe.wait(mark("hT_lo", (b, c // 4)), *wq_ok)
                project("q_mm", b, hT, (wq_hi, wq_lo), (c,), [
                    (mark("q_lo", (b - 1, half)), mark("o", (b - 3, half)), mark("yT_lo", (B - 1, half)))
                    for half in range(2)])

        def split_q(b):
            if not in_range(b):
                return
            for half in range(2):
                src = bank(half).rearrange("p (r n) -> p r n", n=2 * HD)
                hi, lo = (q_split[:, half * PAIRS // 2:(half + 1) * PAIRS // 2, part, :] for part in range(2))
                act.wait(mark("q_mm", (b, "half", half)), mark("qT_mm", (b - 1, 2 * half + 1)))
                m = act.do(lambda e, hi=hi, src=src: e.copy(hi, src), S["q_hi"])
                dve.wait(m)
                M["q_lo", (b, half)] = dve.do(lambda e, hi=hi, lo=lo, src=src: e.tensor_tensor(
                    lo, src, f32(hi), ALU.subtract), S["q_lo"])

        def project_o(b, c):
            if in_range(b):
                pe.wait(mark("c_lo", (b, c // GROUP)), M["wo_in", c // 4])
                project("o_mm", b, cT, (wo_hi, wo_lo), (c,), [
                    (mark("q_lo", (b + 2, half)), mark("q_lo", (B - 1, half)), mark("o", (b - 1, half)))
                    for half in range(2)])

        def finish_out(b):
            if in_range(b):
                dve.wait(M["h_res", b])
                for half in range(2):
                    dve.wait(mark("o_mm", (b, "half", half)))
                    part = h_in[:, half * BANK:(half + 1) * BANK]
                    M["o", (b, half)] = dve.do(lambda e, part=part, half=half: e.tensor_tensor(
                        part, bank(half), part, ALU.add), S["o"])
                sp.wait(mark("o", (b, 1)))
                M["out", b] = sp.do(lambda e: e.dma_start(out[b], h_in[:]), s_out, DMA)

        total = B * UNITS

        def scores(t):
            if not 0 <= t < total:
                return
            b, u = divmod(t, UNITS)
            q = u // GROUP
            pe.wait(mark("qT", (b, u // 2)), mark("kd", (b, q)), mark("exp", t - 2))
            for pair in range(2):
                for kpart in range(2):
                    m = pe.do(lambda e, pair=pair, kpart=kpart: e.matmul(
                        score_bank(t)[:, pair * 2 * P:(pair + 1) * 2 * P], qT[:, 2 * u + pair, :],
                        k_diag[:, q, pair, kpart, :, :].rearrange("p g t -> p (g t)"),
                        start=kpart == 0, stop=kpart == 1), S["sc_mm"] if pair and kpart else None)
            M["sc_mm", t] = m

        def maxima(t):
            if not 0 <= t < total:
                return
            st_t = soft[t % 2]
            dve.wait(mark("sc_mm", t), mark("exp", t - 2))
            m = dve.do(lambda e: e.tensor_reduce(
                st_t[:, 0, :], score_bank(t).rearrange("p (g t) -> p g t", g=GQ), AX_X, ALU.max), S["max"])
            dve.wait(m)
            M["neg", t] = dve.do(lambda e: e.tensor_scalar(st_t[:, 1, :], st_t[:, 0, :], -SCORE1, None, ALU.mult),
                                 S["neg"])

        def exponents(t):
            if not 0 <= t < total:
                return
            st_t = soft[t % 2]
            act.wait(mark("neg", t), mark("pT_mm", t - 2), mark("norm", t - 2))
            for g in range(GQ):
                m = act.do(lambda e, g=g: e.activation(
                    prob[t % 2][:, g, :], score_bank(t)[:, g * P:(g + 1) * P], ACT.Exp,
                    bias=st_t[:, 1, g:g + 1], scale=SCORE1, accum_out=st_t[:, 2, g:g + 1]), S["exp"])
            M["exp", t] = m

        def normalise(t):
            if not 0 <= t < total:
                return
            st_t = soft[t % 2]
            dve.wait(mark("exp", t))
            m = dve.do(lambda e: e.reciprocal(st_t[:, 3, :], st_t[:, 2, :]), S["rec"])
            dve.wait(m)
            M["norm", t] = dve.do(lambda e: e.tensor_tensor(
                prob[t % 2][:], prob[t % 2][:], st_t[:, 3, :, None].to_broadcast([P, GQ, P]), ALU.mult), S["norm"])

        def turn_prob(t):
            if not 0 <= t < total:
                return
            pe.wait(mark("norm", t), mark("pT", t - 2))
            for g in range(GQ):
                m = pe.do(lambda e, g=g: e.transpose(
                    bank(4 + t % 2)[:, g * P:(g + 1) * P], prob[t % 2][:, g, :], ident[:]),
                    S["pT_mm"] if g == GQ - 1 else None)
            M["pT_mm", t] = m

        def evacuate_probT(t):
            if not 0 <= t < total:
                return
            quad, member = divmod(t, GROUP)
            act.wait(mark("pT_mm", t), mark("pv_mm", divmod(quad - 2, NQ)))
            M["pT", t] = act.do(lambda e: e.copy(
                probT[quad % 2][:, member, :, :].rearrange("p g n -> p (g n)"), bank(4 + t % 2)), S["pT"])

        def context(quad):
            if not 0 <= quad < B * NQ:
                return
            b, q = divmod(quad, NQ)
            pe.wait(mark("pT", quad * GROUP + GROUP - 1), M["v_in", (b, q)], mark("c_lo", divmod(quad - 1, NQ)))
            for g in range(GQ):
                m = pe.do(lambda e, g=g: e.matmul(
                    bank(6)[g * HD:(g + 1) * HD, :], v_in[:, q, g, :], probT[quad % 2][:, :, g, :],
                    start=True, stop=True), S["pv_mm"] if g == GQ - 1 else None)
            M["pv_mm", (b, q)] = m

        def split_context(quad):
            if not 0 <= quad < B * NQ:
                return
            b, q = divmod(quad, NQ)
            dst = [cT[:, part, q * GROUP:(q + 1) * GROUP, :].rearrange("p j n -> p (j n)") for part in range(2)]
            act.wait(mark("pv_mm", (b, q)), mark("o_mm", (b - 1, (q + 1) * GROUP - 1)))
            M["c_hi", (b, q)] = act.do(lambda e: e.copy(dst[0], bank(6)), S["c_hi"])
            dve.wait(mark("c_hi", (b, q)))
            M["c_lo", (b, q)] = dve.do(lambda e: e.tensor_tensor(dst[1], bank(6), f32(dst[0]), ALU.subtract),
                                       S["c_lo"])

        TURNS = {0: (("q", 0, 2),), 1: (("q", 0, 3),), 4: (("h", 2, 0),), 5: (("h", 2, 1),),
                 6: (("q", 1, 0),), 7: (("q", 1, 1),)}
        FIRST_TURNS = {0: (("q", 0, 2),), 1: (("q", 0, 3),), 6: (("q", 1, 0), ("h", 2, 0)),
                       7: (("q", 1, 1), ("h", 2, 1))}
        FIRST_CHUNKS = {1: (2,), 2: (3,), 3: (4,), 4: (5,), 5: (6, 7)}
        LAST_CHUNKS = {(-1, 2): (0,), (-1, 3): (1,), (-1, 4): (2,), (-1, 5): (3,), (-1, 6): (4, 5), (-1, 7): (6, 7),
                       (0, 0): (0, 1), (0, 1): (2, 3), (0, 2): (4, 5), (0, 3): (6, 7)}

        def load_wo(part, chunks):
            for c in chunks:
                M["wo_in", c // 4] = load(f32((wo_hi, wo_lo)[part][:, c, :]), wo_dram[part][c], s_wo_in[c // 4])

        def slot(t):
            b, s = divmod(t, UNITS)
            scores(t)
            turn_prob(t - 2)
            quad_done = (t - GROUP - 2) // GROUP if (t - 2) % GROUP == 0 else None
            if quad_done is not None:
                context(quad_done)
            maxima(t)
            normalise(t - 1)
            evacuate_probT(t - 2)
            for kind, ahead, part in (FIRST_TURNS if b == 0 else TURNS).get(s, ()):
                if kind == "q":
                    turn_q(b + ahead, part)
                    evacuate_qT(b + ahead, part)
                else:
                    turn_h(b + ahead, part)
                    split_hT(b + ahead, part)
            exponents(t)
            if quad_done is not None:
                split_context(quad_done)
            if b >= B - 1:
                for c in LAST_CHUNKS.get((b - B, s), ()):
                    project_o(b - 1, c)
            elif b == 0:
                for c in FIRST_CHUNKS.get(s, ()):
                    project_q(b + 1, c)
            else:
                for c in (2 * (s % 4), 2 * (s % 4) + 1):
                    if s < 4:
                        project_q(b + 1, c)
                    else:
                        project_o(b - 1, c)
            if s == 0:
                keys_diagonal(b, 1)
                load_k(b + 1)
            if s == 3:
                load_v(b, 1)
            if b == 0 and s < 4:
                load_wo(1, (2 * s, 2 * s + 1))
            if s == (5 if b == 0 else 3):
                split_q(b + 1)
            if s == 4:
                keys_diagonal(b + 1, 0)
            if s == 5 and b < B:
                load_h_res(b - 1)
            if s == 7:
                load_v(b + 1, 0)
            if s == (7 if b < B else 3):
                finish_out(b - 1)
                load_h_early(b + 3)
                if b == B - 1:
                    load_h_res(b)

        for b in range(B):
            sequence_a(b)
        assert next_unit[0] == len(units)

        early = [mark("kv_mm", B - 1), mark("gram_mm", B - 1), mark("yT_mm", (B - 1, 1)),
                 mark("yT_lo", (B - 1, 1)), mark("ysum", B - 1), mark("kv", B - 1)]
        for lane in (act, dve, pool, sp):
            lane.wait(*early)
        in_turn(pool, lambda e: e.memset(k_diag[:].bitcast(F32), 0.0), s_pool)
        load_h_early(1)
        load_k(0)

        finish_prepare()
        turn_k(B - 1)
        evacuate_kT(B - 1)
        partition_stats(B - 1)
        for c in range(4):
            project_q(0, c)
        mean_product(B - 1)
        deviation(B - 1)
        project_q(0, 4)
        var_product(B - 1)
        norm_factors(B - 1)
        norm_scale(B - 1)
        for c in range(5, NC):
            project_q(0, c)
        write_h(B - 1)
        split_q(0)

        sp.wait(*o_stored)
        load_wo(0, range(early_wo))
        keys_diagonal(0, 0)
        load_v(0, 0)
        turn_h(1, 0)
        split_hT(1, 0)
        turn_q(0, 0)
        evacuate_qT(0, 0)
        project_q(1, 0)
        turn_h(1, 1)
        split_hT(1, 1)
        load_h_early(2)
        project_q(1, 1)
        turn_q(0, 1)
        evacuate_qT(0, 1)
        late = [mark(n, B - 1) for n in ("kT_mm", "n1_mm", "mx_mm", "st2_mm", "mix_mm", "kT", "h", "gbi", "x_lo",
                                         "mix_lo")]
        late += [(s_prep_lo, s_prep_lo.count), (s_prep_hi, s_prep_hi.count)]
        late += [h_stored[B - 2], h_stored[B - 1], kv_stored[B - 2], kv_stored[B - 1], *o_stored]
        for lane in (pe, act, dve, pool, sp):
            lane.wait(*late)
        load_wo(0, range(early_wo, NC))
        for t in range(total + UNITS // 2):
            slot(t)
        sp.wait(M["out", B - 1])

        with nc.Block() as block:
            @block.tensor
            def _(eng):
                pe.play(eng)

            @block.scalar
            def _(eng):
                act.play(eng)

            @block.vector
            def _(eng):
                dve.play(eng)

            @block.gpsimd
            def _(eng):
                pool.play(eng)

            @block.sync
            def _(eng):
                sp.play(eng)


_INS = ["x", "ctx_4096",
        "L0_xattn_Wq", "L0_xattn_bq", "L0_xattn_Wk", "L0_xattn_bk", "L0_xattn_Wv", "L0_xattn_bv",
        "L0_xattn_Wo", "L0_xattn_bo", "L0_xattn_gn_w", "L0_xattn_gn_b",
        "L1_xattn_Wq", "L1_xattn_Aq", "L1_xattn_Bq", "L1_xattn_Wk", "L1_xattn_Ak", "L1_xattn_Bk",
        "L1_xattn_Wv", "L1_xattn_Av", "L1_xattn_Bv", "L1_xattn_Wo", "L1_xattn_Ao", "L1_xattn_Bo"]


def kernel(**inputs):
    import numpy as np
    import concourse.bacc as bacc
    from concourse.bass_utils import run_bass_kernel_spmd

    nc = bacc.Bacc("TRN2", target_bir_lowering=False, num_devices=1)
    arrays, args = {}, []
    for name in _INS:
        a = np.ascontiguousarray(inputs[name])
        arrays[f"in_{name}"] = a
        args.append(nc.dram_tensor(f"in_{name}", a.shape, mybir.dt.from_np(a.dtype), kind="ExternalInput").ap())
    shape = arrays["in_x"].shape
    out = nc.dram_tensor("out_dram", shape, F32, kind="ExternalOutput").ap()
    xattn_two_layers(nc, *args, out)
    result = run_bass_kernel_spmd(nc, [arrays], core_ids=[0])
    return result.results[0]["out_dram"]
```
